# Optimizing a Trainium2 kernel written in Bass

```python
import numpy as np
import jax
import jax.numpy as jnp

def _softmax(x, axis=-1):
    return jax.nn.softmax(x, axis=axis)

def _gelu(x):
    return jax.nn.gelu(x, approximate=True)

def _silu(x):
    return jax.nn.silu(x)

def _sigmoid(x):
    return jax.nn.sigmoid(x)

def _layernorm(x, axis=-1, eps=1e-05):
    m = jnp.mean(x, axis=axis, keepdims=True)
    v = jnp.var(x, axis=axis, keepdims=True)
    return (x - m) / jnp.sqrt(v + eps)

def _scatter_add(tgt, idx, src, axis=0):
    return tgt.at[idx].add(src)

def _segment_sum(src, seg, n):
    return jax.ops.segment_sum(src, seg, n)
kernel_name = 'mk_xattn_seq_d2_seqx_r4_de43a6'

def setup_inputs(seed: int=0):
    np.random.seed(seed)
    _w = jnp.asarray

    def _rec_inputs():
        import jax
        import jax.numpy as jnp
        _rk = jax.random.key(seed)
        x = -0.0002928 + 1 * jax.random.normal(jax.random.fold_in(_rk, 1), (16, 128, 256), jnp.float32)
        _lenS = 128 - jax.random.randint(jax.random.fold_in(_rk, 7), (16,), 0, max(1, 128 // 4) + 1, jnp.int32)
        _lenS2 = 128 - jax.random.randint(jax.random.fold_in(_rk, 8), (16,), 0, max(1, 128 // 4) + 1, jnp.int32)
        _ctx_768P = jax.random.normal(jax.random.fold_in(_rk, 11), (16, 16, 192), jnp.float32)
        _ctx_768c = jax.random.dirichlet(jax.random.fold_in(_rk, 511), 0.3 * jnp.ones((16,), jnp.float32), (16, 128))
        _ctx_768t = jnp.einsum('bsk,bkd->bsd', _ctx_768c, _ctx_768P)
        _ctx_768t = _ctx_768t * jax.lax.rsqrt(jnp.mean(jnp.square(_ctx_768t)) + 1e-12) * 0.953939
        ctx_768 = 2.09791e-05 + 1.00001 * (_ctx_768t + 0.3 * jax.random.normal(jax.random.fold_in(_rk, 611), (16, 128, 192), jnp.float32))
        return (x, ctx_768)
    x, ctx_768 = _rec_inputs()

    def _L0_xattn_setup():
        import jax, jax.numpy as jnp
        import numpy as np
        DIM1, DIM2, H = (256, 192, 16)
        HID = 4 * DIM1
        EPS = 1e-05

        def layernorm(x, w, b):
            mu = jnp.mean(x, axis=-1, keepdims=True)
            var = jnp.mean((x - mu) ** 2, axis=-1, keepdims=True)
            return (x - mu) * jax.lax.rsqrt(var + EPS) * w + b
        key = jax.random.key(seed)
        ks = jax.random.split(key, 12)
        s1 = 1.0 / np.sqrt(DIM1)
        s2 = 1.0 / np.sqrt(DIM2)
        sh = 1.0 / np.sqrt(HID)
        return {'x': jax.random.normal(ks[0], (4, 256, DIM1), jnp.float32), 'y': jax.random.normal(ks[1], (4, 256, DIM2), jnp.float32), 'ln1_w': jnp.ones((DIM1,), jnp.float32), 'ln1_b': jnp.zeros((DIM1,), jnp.float32), 'ln2_w': jnp.ones((DIM2,), jnp.float32), 'ln2_b': jnp.zeros((DIM2,), jnp.float32), 'ln3_w': jnp.ones((DIM1,), jnp.float32), 'ln3_b': jnp.zeros((DIM1,), jnp.float32), 'Wq': jax.random.uniform(ks[2], (DIM1, DIM1), jnp.float32, -s1, s1), 'Wkv': jax.random.uniform(ks[3], (DIM2, 2 * DIM1), jnp.float32, -s2, s2), 'Wproj': jax.random.uniform(ks[4], (DIM1, DIM1), jnp.float32, -s1, s1), 'bproj': jnp.zeros((DIM1,), jnp.float32), 'W1': jax.random.uniform(ks[5], (DIM1, HID), jnp.float32, -s1, s1), 'b1': jnp.zeros((HID,), jnp.float32), 'W2': jax.random.uniform(ks[6], (HID, DIM1), jnp.float32, -sh, sh), 'b2': jnp.zeros((DIM1,), jnp.float32)}
    _L0_xattn_all = _L0_xattn_setup()
    _L0_xattn_in = {k: v for k, v in _L0_xattn_all.items() if k in ('ln1_w', 'ln1_b', 'ln2_w', 'ln2_b', 'ln3_w', 'ln3_b', 'Wq', 'Wkv', 'Wproj', 'bproj', 'W1', 'b1', 'W2', 'b2')}
    del _L0_xattn_all

    def _L1_xattn_setup():
        import jax, jax.numpy as jnp
        import numpy as np
        EPS_RMS = 1e-05
        EPS_L2 = 1e-12
        MAX_SEQ_LEN = 1024
        D_Q, D_KV, N_HEADS = (256, 192, 16)
        HEAD_DIM = D_Q // N_HEADS

        def _rope_tables(head_dim, max_len):
            inv_freq = 1.0 / 10000.0 ** (np.arange(0, head_dim, 2, dtype=np.float32) / head_dim)
            t = np.arange(max_len, dtype=np.float32)
            freqs = np.einsum('i,j->ij', t, inv_freq)
            emb = np.concatenate([freqs, freqs], axis=-1)
            return (jnp.asarray(np.cos(emb)), jnp.asarray(np.sin(emb)))

        def _rotate(x, cos, sin):
            T = x.shape[1]
            c = cos[:T][None, :, None, :]
            s = sin[:T][None, :, None, :]
            x1, x2 = jnp.split(x, 2, axis=-1)
            return x * c + jnp.concatenate([-x2, x1], axis=-1) * s
        key = jax.random.key(seed)
        ks = jax.random.split(key, 6)
        B, T_dec, T_enc = (4, 128, 512)
        x = jax.random.normal(ks[0], (B, T_dec, D_Q), dtype=jnp.float32)
        encoder_out = jax.random.normal(ks[1], (B, T_enc, D_KV), dtype=jnp.float32)
        sq = 1.0 / np.sqrt(D_Q)
        skv = 1.0 / np.sqrt(D_KV)
        norm_w = jnp.ones((D_Q,), dtype=jnp.float32)
        wq = jax.random.normal(ks[2], (D_Q, D_Q), dtype=jnp.float32) * sq
        wkv = jax.random.normal(ks[3], (D_KV, 2 * D_Q), dtype=jnp.float32) * skv
        wout = jax.random.normal(ks[4], (D_Q, D_Q), dtype=jnp.float32) * sq
        return {'x': x, 'encoder_out': encoder_out, 'norm_w': norm_w, 'wq': wq, 'wkv': wkv, 'wout': wout}
    _L1_xattn_all = _L1_xattn_setup()
    _L1_xattn_in = {k: v for k, v in _L1_xattn_all.items() if k in ('norm_w', 'wq', 'wkv', 'wout')}
    del _L1_xattn_all
    return {'x': x, 'ctx_768': ctx_768, 'L0_xattn_ln1_w': _L0_xattn_in['ln1_w'], 'L0_xattn_ln1_b': _L0_xattn_in['ln1_b'], 'L0_xattn_ln2_w': _L0_xattn_in['ln2_w'], 'L0_xattn_ln2_b': _L0_xattn_in['ln2_b'], 'L0_xattn_ln3_w': _L0_xattn_in['ln3_w'], 'L0_xattn_ln3_b': _L0_xattn_in['ln3_b'], 'L0_xattn_Wq': _L0_xattn_in['Wq'], 'L0_xattn_Wkv': _L0_xattn_in['Wkv'], 'L0_xattn_Wproj': _L0_xattn_in['Wproj'], 'L0_xattn_bproj': _L0_xattn_in['bproj'], 'L0_xattn_W1': _L0_xattn_in['W1'], 'L0_xattn_b1': _L0_xattn_in['b1'], 'L0_xattn_W2': _L0_xattn_in['W2'], 'L0_xattn_b2': _L0_xattn_in['b2'], 'L1_xattn_norm_w': _L1_xattn_in['norm_w'], 'L1_xattn_wq': _L1_xattn_in['wq'], 'L1_xattn_wkv': _L1_xattn_in['wkv'], 'L1_xattn_wout': _L1_xattn_in['wout']}

def reference(x, ctx_768, L0_xattn_ln1_w, L0_xattn_ln1_b, L0_xattn_ln2_w, L0_xattn_ln2_b, L0_xattn_ln3_w, L0_xattn_ln3_b, L0_xattn_Wq, L0_xattn_Wkv, L0_xattn_Wproj, L0_xattn_bproj, L0_xattn_W1, L0_xattn_b1, L0_xattn_W2, L0_xattn_b2, L1_xattn_norm_w, L1_xattn_wq, L1_xattn_wkv, L1_xattn_wout):
    import jax
    import jax.numpy as jnp

    def _L0_xattn_ref(x, y, ln1_w, ln1_b, ln2_w, ln2_b, ln3_w, ln3_b, Wq, Wkv, Wproj, bproj, W1, b1, W2, b2):
        import jax, jax.numpy as jnp
        import numpy as np
        DIM1, DIM2, H = (256, 192, 16)
        HID = 4 * DIM1
        EPS = 1e-05

        def layernorm(x, w, b):
            mu = jnp.mean(x, axis=-1, keepdims=True)
            var = jnp.mean((x - mu) ** 2, axis=-1, keepdims=True)
            return (x - mu) * jax.lax.rsqrt(var + EPS) * w + b
        B, N1, C1 = x.shape
        hd = C1 // H
        scale = hd ** (-0.5)
        xn = layernorm(x, ln1_w, ln1_b)
        yn = layernorm(y, ln2_w, ln2_b)
        q = (xn @ Wq).reshape(B, N1, H, hd).transpose(0, 2, 1, 3)
        kv = (yn @ Wkv).reshape(B, y.shape[1], 2, H, hd)
        k = kv[:, :, 0].transpose(0, 2, 1, 3)
        v = kv[:, :, 1].transpose(0, 2, 1, 3)
        attn = jax.nn.softmax(jnp.einsum('bhqd,bhkd->bhqk', q, k) * scale, axis=-1)
        o = jnp.einsum('bhqk,bhkd->bhqd', attn, v).transpose(0, 2, 1, 3).reshape(B, N1, C1)
        x = x + (o @ Wproj + bproj)
        h = jax.nn.gelu(layernorm(x, ln3_w, ln3_b) @ W1 + b1, approximate=False)
        x = x + (h @ W2 + b2)
        return x

    def _L1_xattn_ref(x, encoder_out, norm_w, wq, wkv, wout):
        import jax, jax.numpy as jnp
        import numpy as np
        EPS_RMS = 1e-05
        EPS_L2 = 1e-12
        MAX_SEQ_LEN = 1024
        D_Q, D_KV, N_HEADS = (256, 192, 16)
        HEAD_DIM = D_Q // N_HEADS

        def _rope_tables(head_dim, max_len):
            inv_freq = 1.0 / 10000.0 ** (np.arange(0, head_dim, 2, dtype=np.float32) / head_dim)
            t = np.arange(max_len, dtype=np.float32)
            freqs = np.einsum('i,j->ij', t, inv_freq)
            emb = np.concatenate([freqs, freqs], axis=-1)
            return (jnp.asarray(np.cos(emb)), jnp.asarray(np.sin(emb)))

        def _rotate(x, cos, sin):
            T = x.shape[1]
            c = cos[:T][None, :, None, :]
            s = sin[:T][None, :, None, :]
            x1, x2 = jnp.split(x, 2, axis=-1)
            return x * c + jnp.concatenate([-x2, x1], axis=-1) * s
        B, T_dec, _ = x.shape
        T_enc = encoder_out.shape[1]
        cos, sin = _rope_tables(HEAD_DIM, MAX_SEQ_LEN)
        residual = x
        xn = x * jax.lax.rsqrt(jnp.mean(x * x, axis=-1, keepdims=True) + EPS_RMS) * norm_w
        q = (xn @ wq).reshape(B, T_dec, N_HEADS, HEAD_DIM)
        kv = (encoder_out @ wkv).reshape(B, T_enc, 2, N_HEADS, HEAD_DIM)
        k, v = (kv[:, :, 0], kv[:, :, 1])
        q = _rotate(q, cos, sin)
        k = _rotate(k, cos, sin)
        q = q / jnp.maximum(jnp.linalg.norm(q, axis=-1, keepdims=True), EPS_L2)
        k = k / jnp.maximum(jnp.linalg.norm(k, axis=-1, keepdims=True), EPS_L2)
        scale = jnp.sqrt(jnp.float32(HEAD_DIM))
        logits = jnp.einsum('bqhd,bkhd->bhqk', q, k) * scale
        attn = jax.nn.softmax(logits, axis=-1)
        out = jnp.einsum('bhqk,bkhd->bqhd', attn, v).reshape(B, T_dec, D_Q)
        return residual + out @ wout
    x = _L0_xattn_ref(x, ctx_768, L0_xattn_ln1_w, L0_xattn_ln1_b, L0_xattn_ln2_w, L0_xattn_ln2_b, L0_xattn_ln3_w, L0_xattn_ln3_b, L0_xattn_Wq, L0_xattn_Wkv, L0_xattn_Wproj, L0_xattn_bproj, L0_xattn_W1, L0_xattn_b1, L0_xattn_W2, L0_xattn_b2)
    x = _L1_xattn_ref(x, ctx_768, L1_xattn_norm_w, L1_xattn_wq, L1_xattn_wkv, L1_xattn_wout)
    return x

_drawn_inputs = setup_inputs


def setup_inputs(seed=0):
    import zlib

    import numpy as np

    out = dict(_drawn_inputs(seed))
    spreads = {'L0_xattn_ln1_w': (1.0, 0.6),
     'L0_xattn_ln1_b': (0.0, 0.8),
     'L0_xattn_ln2_w': (1.0, 0.6),
     'L0_xattn_ln2_b': (0.0, 0.1),
     'L0_xattn_ln3_w': (1.0, 0.2),
     'L0_xattn_ln3_b': (0.0, 0.432),
     'L0_xattn_bproj': (0.0, 0.1),
     'L0_xattn_b1': (0.0, 0.294),
     'L0_xattn_b2': (0.0, 0.1),
     'L1_xattn_norm_w': (1.0, 0.6)}
    factors = {'L0_xattn_Wq': 3.159}
    for name, (base, spread) in spreads.items():
        noise = np.random.default_rng([zlib.crc32(name.encode()), seed]).standard_normal(out[name].shape)
        drawn = base * np.exp(spread * noise) if base else spread * noise
        out[name] = jnp.asarray(drawn.astype(out[name].dtype))
    for name, factor in factors.items():
        out[name] = (out[name] * factor).astype(out[name].dtype)
    return out
```

```python
import concourse.bass as bass
from concourse import mybir
from contextlib import ExitStack

fp32 = mybir.dt.float32
ALU = mybir.AluOpType
ACT = mybir.ActivationFunctionType
AX = mybir.AxisListType

NB, TOK, C1, C2, H = 16, 128, 256, 192, 16
HD = C1 // H
HID = 4 * C1
KT = C1 // 128
C2B = C2 - 128
NG = 4
GH = H // NG
MH = 128 // HD
VW = HD + 1
HM = HID // 128
NP = NB // 2
EPS = 1e-5
EPS_L2 = 1e-12
LOADED = 16
SCATTER = MH * LOADED


def pipeline(eng, step, peeled=4):
    def one(s):
        step(s // 2, s % 2, s < NB, 2 <= s < NB + 2, 3 <= s)
    for s in range(peeled):
        one(s)
    with eng.Fori(0, (NB - peeled) // 2) as i:
        for j in range(2):
            step(i + peeled // 2, j, True, True, True)
    for s in range(NB, NB + 3):
        one(s)


def build(nc, x, ctx, ln1_w, ln1_b, ln2_w, ln2_b, ln3_w, ln3_b, Wq, Wkv, Wproj, bproj, W1, b1, W2, b2,
          norm_w, wq, wkv, wout, rope, out):
    es = ExitStack()
    with es:
        def sb(name, *shape):
            return es.enter_context(nc.sbuf_tensor(name, list(shape), fp32))

        def ps(name):
            return es.enter_context(nc.psum_tensor(name, [128, 512], fp32))

        def sem(name):
            return es.enter_context(nc.semaphore(name))

        ident = sb("ident", 128, 128)
        eps_t = sb("eps_t", 128, 2)
        minus_half = sb("minus_half", 128, 2 * H)
        x_all = sb("x_all", 128, NB, C1)
        ctx_in = sb("ctx_in", 128, 2, C2)
        xn = sb("xn", 128, 2, C1)
        yn = sb("yn", 128, 2, C2)
        inT = sb("inT", 128, 2, 4, TOK)
        qkT = sb("qkT", 128, 2, 4, TOK)
        kmask = sb("kmask", 128, 2, H, TOK)
        vals = sb("vals", 128, 2, H, VW)
        P = sb("P", 128, 2, 512)
        PT = sb("PT", 128, 4, 512)
        oT = sb("oT", 128, 512)
        on = sb("on", 128, C1)
        onT = sb("onT", 128, KT, TOK)
        row_sums_inv = sb("row_sums_inv", 128, H)
        row_max = sb("row_max", 128, NG, GH)
        stats = sb("stats", 128, 2, 12)
        wait_carrier = sb("wait_carrier", 128, 1)
        mean_var = sb("mean_var", 128, 2, 4)
        var_eps = sb("var_eps", 128, 2, 2)
        rstd = sb("rstd", 128, 2, 2)
        Wq_s = sb("Wq_s", 128, KT, C1)
        Wkv_s = sb("Wkv_s", 128, 2, 2 * C1)
        Wproj_s = sb("Wproj_s", 128, KT, C1)
        W1_s = sb("W1_s", 128, KT, HID)
        W2_s = sb("W2_s", 128, HM, C1)
        wq_s = sb("wq_s", 128, KT, C1)
        wkv_s = sb("wkv_s", 128, 2, 2 * C1)
        wout_s = sb("wout_s", 128, KT, C1)
        ln_cols = sb("ln_cols", 128, 7, KT)
        b1_cols = sb("b1_cols", 128, HM)
        b1_all = sb("b1_all", 128, HM)
        ln2b_wide = sb("ln2b_wide", 128, 2, 128)
        qk_bias = sb("qk_bias", 128, 4)
        v_bias = sb("v_bias", 128, C1)
        bproj_row = sb("bproj_row", 128, C1)
        b2_row = sb("b2_row", 128, C1)
        rope_t = sb("rope_t", 128, 2, HD)
        lnT = sb("lnT", 128, KT, 2 * TOK)
        hT = sb("hT", 128, HM, 2 * TOK)
        mean_sq = sb("mean_sq", 128, 2, 1)
        x_sq = sb("x_sq", 128, C1)
        rot_a = sb("rot_a", 128, 2 * C1)
        rot_b = sb("rot_b", 128, 2 * C1)
        rot = sb("rot", 128, 2, 2 * C1)
        rot_sq = sb("rot_sq", 128, 2 * C1)
        norm_sq = sb("norm_sq", 128, 2, 2 * H)
        norm_sq_min = sb("norm_sq_min", 128, 2, 2 * H)
        norm_inv = sb("norm_inv", 128, 2, 2 * H)
        qk_unit = sb("qk_unit", 128, 2 * C1)
        y_out = sb("y_out", 128, 2, C1)

        bank_s = [ps(f"bank_s{n}") for n in range(4)]
        bank_o = ps("bank_o")
        bank_y = ps("bank_y")
        bank_t = ps("bank_t")
        bank_qk = ps("bank_qk")

        in_loaded = [sem(f"in_loaded{j}") for j in range(2)]
        w_att_loaded, w_out_loaded, w_mlp_loaded, w_b1_loaded = sem("w_att"), sem("w_out"), sem("w_mlp"), sem("w_b1")
        const_ready, ident_ready, zero_ready = sem("const_ready"), sem("ident_ready"), sem("zero_ready")
        wide_ready, bias_mm, w_att_ready, w_mlp_ready = sem("wide_ready"), sem("bias_mm"), sem("w_att_ready"), sem("w_mlp_ready")

        def att_sems(n):
            names = ("stats_raw", "stats_ready", "var_ready", "rstd_ready", "norm_done", "in_transposed", "inT_ready",
                     "qk_mm", "qk_ready", "v_mm", "v_ready", "scores", "maxed", "shifted", "exped", "w_transposed",
                     "wT_ready", "av", "oT_ready", "o_back", "recip", "on_ready", "on_transposed", "onT_ready",
                     "proj_mm", "res_ready", "bias_added")
            return {k: sem(f"{n}_{k}") for k in names}

        A, C = att_sems("a"), att_sems("c")
        a_scattered = [sem(f"a_scattered{j}") for j in range(2)]
        c_scattered = [sem(f"c_scattered{j}") for j in range(2)]
        c_loaded = [sem(f"c_loaded{j}") for j in range(2)]
        c_stored = [sem(f"c_stored{j}") for j in range(2)]
        c_rope, c_turned, c_rot, c_rot_sq, c_norm_sq, c_norm_min, c_norm_inv, c_unit, c_unit_T = (
            sem(f"c_{k}") for k in ("rope", "turned", "rot", "rot_sq", "norm_sq", "norm_min", "norm_inv", "unit", "unit_T"))
        b_stats_raw, b_stats, b_var, b_rstd, b_norm, b_bias, b_T, b_lnT, b_w1, b_gelu, b_w2, b_x = (
            sem(f"b_{k}") for k in ("stats_raw", "stats", "var", "rstd", "norm", "bias", "T", "lnT", "w1", "gelu", "w2", "x"))

        block = es.enter_context(nc.Block())

        def tile_of(t):
            return x_all[:, bass.ds(t, 1), :].rearrange("p b c -> p (b c)")

        def heads(ap, n=H):
            return ap.rearrange("p (h d) -> p h d", h=n)

        def each(col, n, width):
            return col.unsqueeze(2).broadcast_to([128, n, width])

        @block.sync
        def _(sp):
            def load_in(t, j, loaded):
                if loaded is in_loaded:
                    sp.dma_start(tile_of(t), x[bass.ds(t, 1)].rearrange("b p c -> p (b c)")).then_inc(loaded[j], LOADED)
                sp.dma_start(ctx_in[:, j, :], ctx[bass.ds(t, 1)].rearrange("b p c -> p (b c)")).then_inc(loaded[j], LOADED)

            def scatter(j, scattered):
                for h in range(MH):
                    r = slice(HD * h, HD * h + HD)
                    sp.dma_start(kmask[r, j, h:H:MH, :], qkT[r, j, 2:4, :]).then_inc(scattered[j], LOADED)

            for j in range(2):
                load_in(j, j, in_loaded)
            sp.dma_start(Wkv_s[:, 0, :], Wkv[0:128, :]).then_inc(w_att_loaded, LOADED)
            sp.dma_start(Wkv_s[0:C2B, 1, :], Wkv[128:C2, :]).then_inc(w_att_loaded, LOADED)
            sp.dma_start(Wq_s[:, :, :], Wq.rearrange("(t p) n -> p t n", p=128)).then_inc(w_att_loaded, LOADED)
            sp.dma_start(Wproj_s[:, :, :], Wproj.rearrange("(t p) n -> p t n", p=128)).then_inc(w_out_loaded, LOADED)
            sp.dma_start(bproj_row[:, :], bproj.unsqueeze(0).broadcast_to([128, C1])).then_inc(w_out_loaded, LOADED)
            sp.dma_start(b2_row[:, :], b2.unsqueeze(0).broadcast_to([128, C1])).then_inc(w_out_loaded, LOADED)
            sp.dma_start(W1_s[:, :, :], W1.rearrange("(t p) n -> p t n", p=128)).then_inc(w_mlp_loaded, LOADED)
            sp.dma_start(W2_s[:, :, :], W2.rearrange("(t p) n -> p t n", p=128)).then_inc(w_mlp_loaded, LOADED)
            sp.dma_start(wq_s[:, :, :], wq.rearrange("(t p) n -> p t n", p=128)).then_inc(w_mlp_loaded, LOADED)
            sp.dma_start(wkv_s[:, 0, :], wkv[0:128, :]).then_inc(w_mlp_loaded, LOADED)
            sp.dma_start(wkv_s[0:C2B, 1, :], wkv[128:C2, :]).then_inc(w_mlp_loaded, LOADED)
            sp.dma_start(wout_s[:, :, :], wout.rearrange("(t p) n -> p t n", p=128)).then_inc(w_mlp_loaded, LOADED)
            sp.wait_ge(zero_ready, 3)

            def step_a(p, j, dense, attend, finish, first=False):
                t = 2 * p + j
                if dense:
                    sp.wait_ge(A["qk_ready"], t + 1)
                    scatter(j, a_scattered)

            def loads_a(p, j, t_next):
                sp.wait_ge(A["norm_done"], 2 * (2 * p + j) + 2)
                load_in(t_next, j, in_loaded)

            for s in range(4):
                loads_a(s // 2, s % 2, s + 2)
                step_a(s // 2, s % 2, True, s >= 2, False)
            with sp.Fori(0, (NB - 6) // 2) as i:
                for j in range(2):
                    loads_a(i + 2, j, 2 * i + 6 + j)
                    step_a(i + 2, j, True, True, True)
            for s in range(NB - 2, NB):
                step_a(s // 2, s % 2, True, True, True)

            sp.wait_ge(A["norm_done"], 2 * NB)
            for j in range(2):
                load_in(j, j, c_loaded)

            def scatter_c(p, j):
                t = 2 * p + j
                sp.wait_ge(c_unit_T, t + 1)
                scatter(j, c_scattered)

            def store(t, j):
                sp.wait_ge(C["res_ready"], t + 1)
                sp.dma_start(out[bass.ds(t, 1)].rearrange("b p c -> p (b c)"), y_out[:, j, :]).then_inc(c_stored[j], LOADED)

            def step_c(p, j, load, turn, finish):
                t = 2 * p + j
                if load:
                    sp.wait_ge(C["in_transposed"], t + 1)
                    load_in(t + 2, j, c_loaded)
                if turn:
                    if j:
                        scatter_c(p, 0)
                    else:
                        scatter_c(p - 1, 1)
                if finish:
                    store(t - 3, 1 - j)

            for s in range(4):
                step_c(s // 2, s % 2, True, s >= 1, s >= 3)
            with sp.Fori(0, (NB - 6) // 2) as i:
                for j in range(2):
                    step_c(i + 2, j, True, True, True)
            for s in range(NB - 2, NB + 3):
                step_c(s // 2, s % 2, False, s <= NB, True)
            for j in range(2):
                sp.wait_ge(c_stored[j], NP * LOADED)

        @block.gpsimd
        def _(pool):
            nc.gpsimd.memset(ident[:, :], 0.0).then_inc(ident_ready, 1)
            nc.gpsimd.memset(minus_half[:, :], -0.5).then_inc(const_ready, 1)
            nc.gpsimd.memset(eps_t[:, :], EPS).then_inc(const_ready, 1)
            pool.wait_ge(ident_ready, 1)
            nc.gpsimd.affine_select(out=ident[:, :], in_=ident[:, :], compare_op=ALU.not_equal, fill=1.0, base=0,
                                    pattern=[[-1, 128]], channel_multiplier=1).then_inc(ident_ready, 1)
            for j in range(2):
                nc.gpsimd.memset(kmask[:, j, :, :], 0.0).then_inc(zero_ready, 1)
            nc.gpsimd.memset(vals[:, :, :, :], 1.0).then_inc(zero_ready, 1)

            def step_a(p, j, dense, attend, finish):
                t = 2 * p + j
                if dense:
                    pool.wait_ge(A["stats_ready"], 2 * t + 2)
                    nc.gpsimd.tensor_tensor(var_eps[:, j, :], mean_var[:, j, 1:4:2], eps_t[:, :], ALU.add)\
                        .then_inc(A["var_ready"], 1)
                    pool.wait_ge(A["var_ready"], t + 1)
                    nc.gpsimd.tensor_tensor(rstd[:, j, :], var_eps[:, j, :], minus_half[:, 0:2], ALU.pow)\
                        .then_inc(A["rstd_ready"], 1)
                    pool.wait_ge(A["norm_done"], 2 * t + 2)
                    nc.gpsimd.tensor_tensor(tile_of(t), tile_of(t), bproj_row[:, :], ALU.add)\
                        .then_inc(A["bias_added"], 1)

            pool.wait_ge(const_ready, 2)
            pool.wait_ge(w_out_loaded, 3 * LOADED)
            pipeline(pool, step_a)

            def norm_b(p):
                pool.wait_ge(b_stats, 2 * p + 2)
                nc.gpsimd.tensor_tensor(var_eps[:, :, 0], mean_var[:, :, 1], eps_t[:, :], ALU.add).then_inc(b_var, 1)
                pool.wait_ge(b_var, p + 1)
                nc.gpsimd.tensor_tensor(rstd[:, :, 0], var_eps[:, :, 0], minus_half[:, 0:2], ALU.pow).then_inc(b_rstd, 1)
                pool.wait_ge(b_norm, 2 * p + 2)
                for j in range(2):
                    nc.gpsimd.tensor_tensor(tile_of(2 * p + j), tile_of(2 * p + j), b2_row[:, :], ALU.add).then_inc(b_bias, 1)

            norm_b(0)
            with pool.Fori(0, NP - 1) as i:
                norm_b(i + 1)

            def step_c(p, j, dense, attend, finish):
                t = 2 * p + j
                if dense:
                    pool.wait_ge(C["stats_ready"], t + 1)
                    nc.gpsimd.tensor_tensor(var_eps[:, j, 0:1], mean_sq[:, j, :], eps_t[:, 0:1], ALU.add)\
                        .then_inc(C["var_ready"], 1)
                    pool.wait_ge(C["var_ready"], t + 1)
                    nc.gpsimd.tensor_tensor(rstd[:, j, 0:1], var_eps[:, j, 0:1], minus_half[:, 0:1], ALU.pow)\
                        .then_inc(C["rstd_ready"], 1)
                    pool.wait_ge(c_norm_min, t + 1)
                    nc.gpsimd.tensor_tensor(norm_inv[:, j, :], norm_sq_min[:, j, :], minus_half[:, :], ALU.pow)\
                        .then_inc(c_norm_inv, 1)

            pipeline(pool, step_c)

        @block.scalar
        def _(act):
            for n, v in enumerate((ln1_w, ln1_b, ln2_w, ln2_b)):
                if n < 2:
                    act.dma_start(ln_cols[:, n, :], v.rearrange("(t p) -> p t", p=128), allow_slow_non_contiguous=True).then_inc(w_att_loaded, LOADED)
                else:
                    act.dma_start(ln_cols[:, n, 0:1], v[0:128].unsqueeze(1)).then_inc(w_att_loaded, LOADED)
                    act.dma_start(ln_cols[0:C2B, n, 1:2], v[128:C2].unsqueeze(1)).then_inc(w_att_loaded, LOADED)
            for n, v in enumerate((ln3_w, ln3_b, norm_w)):
                act.dma_start(ln_cols[:, 4 + n, :], v.rearrange("(t p) -> p t", p=128), allow_slow_non_contiguous=True).then_inc(w_b1_loaded, LOADED)
            act.dma_start(b1_cols[:, :], b1.rearrange("(t p) -> p t", p=128), allow_slow_non_contiguous=True).then_inc(w_b1_loaded, LOADED)
            act.dma_start(rope_t[:, :, :], rope).then_inc(w_b1_loaded, LOADED)

            def inputs_T(t, j, old, S):
                act.wait_ge(S["in_transposed"], t + 1)
                if old:
                    act.wait_ge(S["v_mm"], t - 1)
                nc.scalar.activation(inT[:, j, 0:3, :], bank_t[:, 0:3 * TOK].rearrange("p (a b) -> p a b", a=3), ACT.Copy)\
                    .then_inc(S["inT_ready"], 1)
                nc.scalar.activation(inT[0:C2B, j, 3, :], bank_t[0:C2B, 3 * TOK:], ACT.Copy).then_inc(S["inT_ready"], 1)

            def out_T(f, later, S):
                act.wait_ge(S["av"], NG * f + NG)
                if later:
                    act.wait_ge(S["o_back"], f)
                nc.scalar.activation(oT[:, :], bank_o[:, :], ACT.Copy).then_inc(S["oT_ready"], 1)

            def on_T(f, later, S):
                act.wait_ge(S["on_transposed"], f + 1)
                if later:
                    act.wait_ge(S["proj_mm"], f)
                nc.scalar.activation(onT[:, :, :], bank_y[:, 0:C1].rearrange("p (a b) -> p a b", a=KT), ACT.Copy)\
                    .then_inc(S["onT_ready"], 1)

            def step_a(p, j, dense, attend, finish):
                t = 2 * p + j
                a, f = t - 2, t - 3

                def exp(g):
                    c = NG * a + g
                    act.wait_ge(A["shifted"], c + 1)
                    nc.scalar.activation(P[:, g % 2, :], P[:, g % 2, :], ACT.Exp, scale=HD ** -0.5)\
                        .then_inc(A["exped"], 1)

                def weights_T(g):
                    c = NG * a + g
                    act.wait_ge(A["w_transposed"], c + 1)
                    if finish or g >= 2:
                        act.wait_ge(A["av"], c - 1)
                    nc.scalar.activation(PT[:, g % 2, :], bank_s[2 + g % 2][:, :], ACT.Copy).then_inc(A["wT_ready"], 1)

                if finish:
                    out_T(f, attend and not (isinstance(f, int) and f == 0) or not attend, A)
                if attend:
                    exp(0)
                    exp(1)
                    weights_T(0)
                if finish:
                    on_T(f, attend and not (isinstance(f, int) and f == 0) or not attend, A)
                if dense:
                    inputs_T(t, j, attend, A)
                if attend:
                    exp(2)
                    weights_T(1)
                    exp(3)
                    weights_T(2)
                    weights_T(3)

            pipeline(act, step_a)

            def lnT_b(p, later):
                act.wait_ge(b_T, p + 1)
                if later:
                    act.wait_ge(b_w1, 4 * p)
                nc.scalar.activation(lnT[:, :, :], bank_t[:, :].rearrange("p (a b) -> p a b", a=KT), ACT.Copy)\
                    .then_inc(b_lnT, 1)

            def gelu_b(p, later):
                for u in range(4):
                    act.wait_ge(b_w1, 4 * p + u + 1)
                    if later and u == 0:
                        act.wait_ge(b_w2, 2 * p)
                    for k in range(2):
                        m = 2 * u + k
                        last = nc.scalar.activation(hT[:, m, :], bank_s[u][:, 256 * k:256 * k + 256], ACT.Gelu,
                                                    bias=b1_all[:, m:m + 1])
                    last.then_inc(b_gelu, 1)

            act.wait_ge(w_mlp_ready, 3)
            lnT_b(0, False)
            gelu_b(0, False)
            with act.Fori(0, NP - 1) as i:
                lnT_b(i + 1, True)
                gelu_b(i + 1, True)

            def step_c(p, j, dense, attend, finish):
                t = 2 * p + j
                a, f = t - 2, t - 3

                def exp(g):
                    c = NG * a + g
                    act.wait_ge(C["scores"], c + 1)
                    if finish:
                        act.wait_ge(C["av"], c - 3)
                    nc.scalar.activation(PT[:, g, :], bank_s[g][:, :], ACT.Exp, scale=HD ** 0.5).then_inc(C["exped"], 1)

                if finish:
                    out_T(f, attend and not (isinstance(f, int) and f == 0) or not attend, C)
                if attend:
                    exp(0)
                    exp(1)
                if finish:
                    on_T(f, attend and not (isinstance(f, int) and f == 0) or not attend, C)
                if attend:
                    exp(2)
                if dense:
                    inputs_T(t, j, attend, C)
                if attend:
                    exp(3)
                if dense:
                    act.wait_ge(c_rot, t + 1)
                    if not (isinstance(t, int) and t == 0):
                        act.wait_ge(c_norm_sq, t)
                    nc.scalar.activation(rot_sq[:, :], rot[:, j, :], ACT.Square).then_inc(c_rot_sq, 1)

            pipeline(act, step_c)

        @block.tensor
        def _(pe):
            mm = nc.tensor.matmul
            pe.wait_ge(w_att_loaded, 9 * LOADED)
            pe.wait_ge(wide_ready, 2)
            rows = (128, C2B)
            for m in range(KT):
                for k in range(KT):
                    mm(bank_qk[:, m:m + 1], Wq_s[:, k, 128 * m:128 * m + 128], ln_cols[:, 1, k:k + 1],
                       start=k == 0, stop=k == KT - 1)
            for m in range(KT):
                for k, r in enumerate(rows):
                    mm(bank_qk[:, 2 + m:3 + m], Wkv_s[0:r, k, 128 * m:128 * m + 128], ln_cols[0:r, 3, k:k + 1],
                       start=k == 0, stop=k == 1)
            for k, r in enumerate(rows):
                last = mm(bank_t[:, 0:C1], ln2b_wide[0:r, k, :], Wkv_s[0:r, k, C1:], start=k == 0, stop=k == 1)
            last.then_inc(bias_mm, 1)
            pe.wait_ge(w_mlp_loaded, 6 * LOADED)
            pe.wait_ge(w_b1_loaded, 5 * LOADED)
            for m in range(HM):
                for k in range(KT):
                    last = mm(bank_y[:, m:m + 1], W1_s[:, k, 128 * m:128 * m + 128], ln_cols[:, 5, k:k + 1],
                              start=k == 0, stop=k == KT - 1)
            last.then_inc(bias_mm, 1)
            pe.wait_ge(w_att_ready, 4)
            pe.wait_ge(w_mlp_ready, 3)
            pe.wait_ge(ident_ready, 2)

            def inputs_T(j, xs, ys, S):
                for k in range(KT):
                    nc.tensor.transpose(bank_t[:, 128 * k:128 * k + 128], xs[:, j, 128 * k:128 * k + 128], ident[:, :])
                nc.tensor.transpose(bank_t[:, 256:384], ys[:, j, 0:128], ident[:, :])
                nc.tensor.transpose(bank_t[0:C2B, 384:512], ys[:, j, 128:C2], ident[:, :]).then_inc(S["in_transposed"], 1)

            def values(j, w, S):
                for k, r in enumerate(rows):
                    last = mm(bank_t[:, 0:C1], inT[0:r, j, 2 + k, :], w[0:r, k, C1:], start=k == 0, stop=k == 1)
                last.then_inc(S["v_mm"], 1)

            def weighted(a, g, j, slot, first, S):
                c = NG * a + g
                pe.wait_ge(S["wT_ready"] if S is A else S["exped"], c + 1)
                if g == 0:
                    pe.wait_ge(S["v_ready"], a + 1)
                    if not first:
                        pe.wait_ge(S["oT_ready"], a)
                for r in range(GH):
                    last = mm(bank_o[32 * r:32 * r + VW, 128 * g:128 * g + 128], vals[:, j, GH * g + r, :],
                              PT[:, slot, 128 * r:128 * r + 128], start=True, stop=True)
                last.then_inc(S["av"], 1)

            def back(f, first, S):
                pe.wait_ge(S["oT_ready"], f + 1)
                if not first:
                    pe.wait_ge(S["res_ready"], f)
                for g in range(NG):
                    last = nc.tensor.transpose(bank_y[:, 128 * g:128 * g + 128], oT[:, 128 * g:128 * g + 128], ident[:, :])
                last.then_inc(S["o_back"], 1)

            def normed_T(f, S):
                pe.wait_ge(S["on_ready"], f + 1)
                for k in range(KT):
                    last = nc.tensor.transpose(bank_y[:, 128 * k:128 * k + 128], on[:, 128 * k:128 * k + 128], ident[:, :])
                last.then_inc(S["on_transposed"], 1)

            def project(f, w, S):
                pe.wait_ge(S["onT_ready"], f + 1)
                for k in range(KT):
                    last = mm(bank_y[:, 0:C1], onT[:, k, :], w[:, k, :], start=k == 0, stop=k == KT - 1)
                last.then_inc(S["proj_mm"], 1)

            def step_a(p, j, dense, attend, finish):
                t = 2 * p + j
                a, f = t - 2, t - 3
                first_f = isinstance(f, int) and f == 0

                def score(g):
                    c = NG * a + g
                    if g == 0:
                        pe.wait_ge(A["qk_ready"], a + 1)
                        pe.wait_ge(a_scattered[j], SCATTER * p)
                    if finish or g >= 2:
                        pe.wait_ge(A["shifted"], c - 1)
                    mm(bank_s[g % 2][:, :], qkT[:, j, g // 2, :], kmask[:, j, GH * g:GH * g + GH, :],
                       start=True, stop=True).then_inc(A["scores"], 1)

                def weights_T(g):
                    c = NG * a + g
                    pe.wait_ge(A["exped"], c + 1)
                    if finish or g >= 2:
                        pe.wait_ge(A["wT_ready"], c - 1)
                    for r in range(GH):
                        last = nc.tensor.transpose(bank_s[2 + g % 2][:, 128 * r:128 * r + 128],
                                                   P[:, g % 2, 128 * r:128 * r + 128], ident[:, :])
                    last.then_inc(A["w_transposed"], 1)

                if attend:
                    score(0)
                    score(1)
                if finish:
                    back(f, first_f, A)
                if attend:
                    weights_T(0)
                    score(2)
                    weighted(a, 0, j, 0, isinstance(a, int) and a == 0, A)
                if finish:
                    normed_T(f, A)
                if dense:
                    pe.wait_ge(A["norm_done"], 2 * t + 2)
                    if not (isinstance(t, int) and t == 0):
                        pe.wait_ge(A["v_ready"], t)
                    inputs_T(j, xn, yn, A)
                if attend:
                    weights_T(1)
                    score(3)
                    weighted(a, 1, j, 1, False, A)
                if finish:
                    project(f, Wproj_s, A)
                if dense:
                    pe.wait_ge(A["inT_ready"], 2 * t + 2)
                    if not (isinstance(t, int) and t == 0):
                        pe.wait_ge(A["qk_ready"], t)
                    for m in range(KT):
                        for k in range(KT):
                            mm(bank_qk[:, 128 * m:128 * m + 128], Wq_s[:, k, 128 * m:128 * m + 128], inT[:, j, k, :],
                               start=k == 0, stop=k == KT - 1)
                    for m in range(KT):
                        for k, r in enumerate(rows):
                            last = mm(bank_qk[:, 256 + 128 * m:384 + 128 * m], Wkv_s[0:r, k, 128 * m:128 * m + 128],
                                      inT[0:r, j, 2 + k, :], start=k == 0, stop=k == 1)
                    last.then_inc(A["qk_mm"], 1)
                if attend:
                    weights_T(2)
                    weighted(a, 2, j, 0, False, A)
                if dense:
                    values(j, Wkv_s, A)
                if attend:
                    weights_T(3)
                    weighted(a, 3, j, 1, False, A)

            pe.wait_ge(w_out_loaded, 3 * LOADED)
            pipeline(pe, step_a)

            pe.wait_ge(A["v_ready"], NB)
            pe.wait_ge(A["shifted"], NG * NB)
            pe.wait_ge(A["wT_ready"], NG * NB)
            pe.wait_ge(A["oT_ready"], NB)
            pe.wait_ge(A["res_ready"], NB)

            def turn_b(p):
                pe.wait_ge(b_norm, 2 * p + 2)
                for k in range(KT):
                    for j in range(2):
                        n = 2 * k + j
                        last = nc.tensor.transpose(bank_t[:, 128 * n:128 * n + 128], xn[:, j, 128 * k:128 * k + 128], ident[:, :])
                last.then_inc(b_T, 1)

            def up_b(p, later):
                pe.wait_ge(b_lnT, p + 1)
                for u in range(4):
                    if later:
                        pe.wait_ge(b_gelu, 4 * p + u - 3)
                    for m in (2 * u, 2 * u + 1):
                        for k in range(KT):
                            last = mm(bank_s[u][:, 256 * (m % 2):256 * (m % 2) + 256], W1_s[:, k, 128 * m:128 * m + 128],
                                      lnT[:, k, :], start=k == 0, stop=k == KT - 1)
                    last.then_inc(b_w1, 1)

            def down_b(p, later):
                for j, bank in enumerate((bank_o, bank_y)):
                    if later:
                        pe.wait_ge(b_x, 2 * p + j - 1)
                    for m in range(HM):
                        if j == 0 and m % 2 == 0:
                            pe.wait_ge(b_gelu, 4 * p + m // 2 + 1)
                        last = mm(bank[:, 0:C1], hT[:, m, 128 * j:128 * j + 128], W2_s[:, m, :], start=m == 0, stop=m == HM - 1)
                    last.then_inc(b_w2, 1)

            turn_b(0)
            up_b(0, False)
            turn_b(1)
            down_b(0, False)
            with pe.Fori(0, NP - 2) as i:
                up_b(i + 1, True)
                turn_b(i + 2)
                down_b(i + 1, True)
            up_b(NP - 1, True)
            down_b(NP - 1, True)

            pe.wait_ge(b_x, NB)
            pe.wait_ge(b_gelu, 4 * NP)

            def step_c(p, j, dense, attend, finish):
                t = 2 * p + j
                a, f = t - 2, t - 3
                first_f = isinstance(f, int) and f == 0
                first_t = isinstance(t, int) and t == 0
                first_a = isinstance(a, int) and a == 0
                turn = dense and not first_t or isinstance(t, int) and t == NB

                def score(g):
                    c = NG * a + g
                    if g == 0:
                        pe.wait_ge(c_unit_T, a + 1)
                        pe.wait_ge(c_scattered[j], SCATTER * p)
                    if not first_a:
                        pe.wait_ge(C["exped"], c - 3)
                    for r in range(GH):
                        last = mm(bank_s[g][:, 128 * r:128 * r + 128], kmask[:, j, GH * g + r, :], qkT[:, j, g // 2, :],
                                  start=True, stop=True)
                    last.then_inc(C["scores"], 1)

                if attend:
                    score(0)
                    score(1)
                if finish:
                    back(f, first_f, C)
                if attend:
                    weighted(a, 0, j, 0, first_a, C)
                    score(2)
                if finish:
                    normed_T(f, C)
                if dense:
                    pe.wait_ge(C["norm_done"], t + 1)
                    pe.wait_ge(c_loaded[j], LOADED * (p + 1))
                    if not first_t:
                        pe.wait_ge(C["v_ready"], t)
                    inputs_T(j, xn, ctx_in, C)
                if attend:
                    weighted(a, 1, j, 1, False, C)
                    score(3)
                if turn:
                    pe.wait_ge(c_unit, t)
                    for n in range(4):
                        last = nc.tensor.transpose(bank_qk[:, 128 * n:128 * n + 128], qk_unit[:, 128 * n:128 * n + 128], ident[:, :])
                    last.then_inc(c_turned, 1)
                if finish:
                    project(f, wout_s, C)
                if dense:
                    pe.wait_ge(C["inT_ready"], 2 * t + 2)
                    if not first_t:
                        pe.wait_ge(c_unit_T, t)
                    for k in range(KT):
                        mm(bank_qk[:, 0:C1], inT[:, j, k, :], wq_s[:, k, :], start=k == 0, stop=k == KT - 1)
                    for k, r in enumerate(rows):
                        last = mm(bank_qk[:, C1:], inT[0:r, j, 2 + k, :], wkv_s[0:r, k, 0:C1], start=k == 0, stop=k == 1)
                    last.then_inc(C["qk_mm"], 1)
                if attend:
                    weighted(a, 2, j, 2, False, C)
                if dense:
                    values(j, wkv_s, C)
                if attend:
                    weighted(a, 3, j, 3, False, C)

            pipeline(pe, step_c)

        @block.vector
        def _(dve):
            v = nc.vector
            v.memset(bank_o[:, :], 0.0).then_inc(wide_ready, 1)
            dve.wait_ge(w_att_loaded, 9 * LOADED)
            for k, r in enumerate((128, C2B)):
                last = v.tensor_copy(ln2b_wide[0:r, k, :], ln_cols[0:r, 3, k:k + 1].broadcast_to([r, 128]))
            last.then_inc(wide_ready, 1)
            dve.wait_ge(bias_mm, 1)
            v.tensor_copy(qk_bias[:, :], bank_qk[:, 0:4]).then_inc(w_att_ready, 1)
            v.tensor_copy(v_bias[:, :], bank_t[:, 0:C1]).then_inc(w_att_ready, 1)
            for k in range(KT):
                last = v.tensor_scalar(Wq_s[:, k, :], Wq_s[:, k, :], ln_cols[:, 0, k:k + 1], None, ALU.mult)
            last.then_inc(w_att_ready, 1)
            for k, r in enumerate((128, C2B)):
                last = v.tensor_scalar(Wkv_s[0:r, k, :], Wkv_s[0:r, k, :], ln_cols[0:r, 2, k:k + 1], None, ALU.mult)
            last.then_inc(w_att_ready, 1)
            dve.wait_ge(bias_mm, 2)
            v.tensor_tensor(b1_all[:, :], bank_y[:, 0:HM], b1_cols[:, :], ALU.add).then_inc(w_mlp_ready, 1)
            for k in range(KT):
                last = v.tensor_scalar(W1_s[:, k, :], W1_s[:, k, :], ln_cols[:, 4, k:k + 1], None, ALU.mult)
            last.then_inc(w_mlp_ready, 1)
            for k in range(KT):
                last = v.tensor_scalar(wq_s[:, k, :], wq_s[:, k, :], ln_cols[:, 6, k:k + 1], None, ALU.mult)
            last.then_inc(w_mlp_ready, 1)

            def values(t, j, old, bias, S):
                dve.wait_ge(S["v_mm"], t + 1)
                if old:
                    dve.wait_ge(S["av"], NG * (t - 1))
                if bias:
                    v.tensor_tensor(vals[:, j, :, 0:HD], heads(bank_t[:, 0:C1]), heads(v_bias[:, :]), ALU.add)\
                        .then_inc(S["v_ready"], 1)
                else:
                    v.tensor_copy(vals[:, j, :, 0:HD], heads(bank_t[:, 0:C1])).then_inc(S["v_ready"], 1)

            def normalise_heads(f, first, S):
                o = bank_y[:, :].rearrange("p (h d) -> p h d", h=H)
                dve.wait_ge(S["o_back"], f + 1)
                v.reciprocal(row_sums_inv[:, :], o[:, :, HD]).then_inc(S["recip"], 1)
                dve.wait_ge(S["recip"], f + 1)
                if not first:
                    dve.wait_ge(S["on_transposed"], f)
                v.tensor_tensor(heads(on[:, :]), o[:, :, 0:HD], each(row_sums_inv[:, :], H, HD), ALU.mult)\
                    .then_inc(S["on_ready"], 1)

            def step_a(p, j, dense, attend, finish):
                t = 2 * p + j
                a, f = t - 2, t - 3
                first_f = isinstance(f, int) and f == 0

                def shift(g):
                    c = NG * a + g
                    s = heads(bank_s[g % 2][:, :], GH)
                    dve.wait_ge(A["scores"], c + 1)
                    v.tensor_reduce(row_max[:, g, :], s, AX.X, ALU.max).then_inc(A["maxed"], 1)
                    dve.wait_ge(A["maxed"], c + 1)
                    if finish or g >= 2:
                        dve.wait_ge(A["w_transposed"], c - 1)
                    v.tensor_tensor(heads(P[:, g % 2, :], GH), s, each(row_max[:, g, :], GH, TOK), ALU.subtract)\
                        .then_inc(A["shifted"], 1)

                if dense:
                    dve.wait_ge(in_loaded[j], 2 * LOADED * (p + 1))
                    v.bn_stats(stats[:, j, 0:6], tile_of(t)).then_inc(A["stats_raw"], 1)
                    v.bn_stats(stats[:, j, 6:12], ctx_in[:, j, :]).then_inc(A["stats_raw"], 1)
                    dve.wait_ge(A["stats_raw"], 2 * t + 2)
                    v.tensor_copy(wait_carrier[:, :], stats[:, j, 0:1])
                    v.bn_aggr(mean_var[:, j, 0:2], stats[:, j, 0:6]).then_inc(A["stats_ready"], 1)
                    v.bn_aggr(mean_var[:, j, 2:4], stats[:, j, 6:12]).then_inc(A["stats_ready"], 1)
                if attend:
                    shift(0)
                    shift(1)
                if finish:
                    normalise_heads(f, first_f, A)
                if dense:
                    dve.wait_ge(A["stats_ready"], 2 * t + 2)
                    dve.wait_ge(A["rstd_ready"], t + 1)
                    if attend:
                        dve.wait_ge(A["in_transposed"], t - 1)
                    v.tensor_scalar(xn[:, j, :], tile_of(t), mean_var[:, j, 0:1], rstd[:, j, 0:1],
                                    ALU.subtract, ALU.mult).then_inc(A["norm_done"], 1)
                    v.tensor_scalar(yn[:, j, :], ctx_in[:, j, :], mean_var[:, j, 2:3], rstd[:, j, 1:2],
                                    ALU.subtract, ALU.mult).then_inc(A["norm_done"], 1)
                if attend:
                    shift(2)
                    shift(3)
                if finish:
                    dve.wait_ge(A["proj_mm"], f + 1)
                    dve.wait_ge(A["bias_added"], f + 1)
                    v.tensor_tensor(tile_of(f), tile_of(f), bank_y[:, 0:C1], ALU.add).then_inc(A["res_ready"], 1)
                if dense:
                    dve.wait_ge(A["qk_mm"], t + 1)
                    if attend:
                        dve.wait_ge(A["scores"], NG * (t - 1))
                        dve.wait_ge(a_scattered[j], SCATTER * p)
                    v.tensor_tensor(qkT[:, j, :, :], bank_qk[:, :].rearrange("p (a b) -> p a b", a=4),
                                    each(qk_bias[:, :], 4, TOK), ALU.add).then_inc(A["qk_ready"], 1)
                    values(t, j, attend, True, A)

            dve.wait_ge(w_att_ready, 4)
            dve.wait_ge(zero_ready, 3)
            pipeline(dve, step_a)

            dve.wait_ge(A["res_ready"], NB)
            dve.wait_ge(A["in_transposed"], NB)

            def norm_b(p, later):
                for j in range(2):
                    v.bn_stats(stats[:, j, 0:6], tile_of(2 * p + j)).then_inc(b_stats_raw, 1)
                dve.wait_ge(b_stats_raw, 2 * p + 2)
                v.tensor_copy(wait_carrier[:, :], stats[:, 0, 0:1])
                for j in range(2):
                    v.bn_aggr(mean_var[:, j, 0:2], stats[:, j, 0:6]).then_inc(b_stats, 1)
                dve.wait_ge(b_stats, 2 * p + 2)
                dve.wait_ge(b_rstd, p + 1)
                if later:
                    dve.wait_ge(b_T, p)
                for j in range(2):
                    v.tensor_scalar(xn[:, j, :], tile_of(2 * p + j), mean_var[:, j, 0:1], rstd[:, j, 0:1],
                                    ALU.subtract, ALU.mult).then_inc(b_norm, 1)

            def res_b(p):
                for j, bank in enumerate((bank_o, bank_y)):
                    dve.wait_ge(b_w2, 2 * p + j + 1)
                    dve.wait_ge(b_bias, 2 * p + j + 1)
                    v.tensor_tensor(tile_of(2 * p + j), tile_of(2 * p + j), bank[:, 0:C1], ALU.add).then_inc(b_x, 1)

            norm_b(0, False)
            with dve.Fori(0, NP - 1) as i:
                norm_b(i + 1, True)
                res_b(i)
            res_b(NP - 1)

            dve.wait_ge(b_x, NB)
            dve.wait_ge(b_T, NP)

            def step_c(p, j, dense, attend, finish):
                t = 2 * p + j
                a, f = t - 2, t - 3
                first_f = isinstance(f, int) and f == 0
                first_t = isinstance(t, int) and t == 0
                turn = dense and not first_t or isinstance(t, int) and t == NB
                if dense:
                    v.scalar_tensor_tensor(x_sq[:, :], tile_of(t), 1.0 / C1, tile_of(t), ALU.mult, ALU.mult,
                                           accum_out=mean_sq[:, j, :]).then_inc(C["stats_ready"], 1)
                    dve.wait_ge(C["stats_ready"], t + 1)
                    dve.wait_ge(C["rstd_ready"], t + 1)
                    if attend:
                        dve.wait_ge(C["in_transposed"], t - 1)
                    v.tensor_scalar(xn[:, j, :], tile_of(t), rstd[:, j, 0:1], None, ALU.mult).then_inc(C["norm_done"], 1)
                if finish:
                    normalise_heads(f, first_f, C)
                if turn:
                    dve.wait_ge(c_norm_inv, t)
                    if not (isinstance(t, int) and t == 1):
                        dve.wait_ge(c_turned, t - 1)
                    v.tensor_tensor(heads(qk_unit[:, :], 2 * H), heads(rot[:, 1 - j, :], 2 * H),
                                    each(norm_inv[:, 1 - j, :], 2 * H, HD), ALU.mult).then_inc(c_unit, 1)
                    dve.wait_ge(c_turned, t)
                    if finish:
                        dve.wait_ge(C["scores"], NG * (t - 2))
                        dve.wait_ge(c_scattered[1 - j], SCATTER * (p if j else p - 1))
                    v.tensor_copy(qkT[:, 1 - j, :, :], bank_qk[:, :].rearrange("p (a b) -> p a b", a=4)).then_inc(c_unit_T, 1)
                if finish:
                    dve.wait_ge(C["proj_mm"], f + 1)
                    if not (isinstance(f, int) and f < 2):
                        dve.wait_ge(c_stored[1 - j], LOADED * (p - 1 if j else p - 2))
                    v.tensor_tensor(y_out[:, 1 - j, :], tile_of(f), bank_y[:, 0:C1], ALU.add).then_inc(C["res_ready"], 1)
                if dense:
                    dve.wait_ge(C["qk_mm"], t + 1)
                    cos = rope_t[:, 0, :].unsqueeze(1).broadcast_to([128, 2 * H, HD])
                    sin = rope_t[:, 1, :].rearrange("p (s d) -> p s d", s=2).unsqueeze(1).broadcast_to([128, 2 * H, 2, HD // 2])
                    swapped = bank_qk[:, :].rearrange("p (h s d) -> p h s d", s=2, d=HD // 2)[:, :, ::-1, :]
                    v.tensor_tensor(heads(rot_a[:, :], 2 * H), heads(bank_qk[:, :], 2 * H), cos, ALU.mult).then_inc(c_rope, 1)
                    v.tensor_tensor(rot_b[:, :].rearrange("p (h s d) -> p h s d", s=2, d=HD // 2), swapped, sin, ALU.mult)\
                        .then_inc(c_rope, 1)
                    dve.wait_ge(c_rope, 2 * t + 2)
                    v.tensor_tensor(rot[:, j, :], rot_a[:, :], rot_b[:, :], ALU.add).then_inc(c_rot, 1)
                    dve.wait_ge(c_rot_sq, t + 1)
                    v.tensor_reduce(norm_sq[:, j, :], heads(rot_sq[:, :], 2 * H), AX.X, ALU.add).then_inc(c_norm_sq, 1)
                    dve.wait_ge(c_norm_sq, t + 1)
                    v.tensor_scalar(norm_sq_min[:, j, :], norm_sq[:, j, :], EPS_L2 ** 2, None, ALU.max).then_inc(c_norm_min, 1)
                    values(t, j, attend, False, C)

            pipeline(dve, step_c, peeled=6)


_INS = ['x', 'ctx_768', 'L0_xattn_ln1_w', 'L0_xattn_ln1_b', 'L0_xattn_ln2_w', 'L0_xattn_ln2_b', 'L0_xattn_ln3_w',
        'L0_xattn_ln3_b', 'L0_xattn_Wq', 'L0_xattn_Wkv', 'L0_xattn_Wproj', 'L0_xattn_bproj', 'L0_xattn_W1',
        'L0_xattn_b1', 'L0_xattn_W2', 'L0_xattn_b2', 'L1_xattn_norm_w', 'L1_xattn_wq', 'L1_xattn_wkv', 'L1_xattn_wout']


def kernel(**inputs):
    import numpy as np
    import concourse.bacc as bacc
    from concourse.bass_utils import run_bass_kernel_spmd

    nc = bacc.Bacc("TRN2", target_bir_lowering=False, num_devices=1)
    arrays, args = {}, []
    for name in _INS:
        a = np.ascontiguousarray(inputs[name])
        arrays[f"in_{name}"] = a
        args.append(nc.dram_tensor(f"in_{name}", a.shape, mybir.dt.from_np(a.dtype), kind="ExternalInput").ap())
    inv_freq = 1.0 / 10000.0 ** (np.arange(0, HD, 2, dtype=np.float32) / HD)
    angles = np.einsum('i,j->ij', np.arange(TOK, dtype=np.float32), inv_freq)
    rope = np.stack([np.cos(np.concatenate([angles, angles], -1)),
                     np.concatenate([-np.sin(angles), np.sin(angles)], -1)], 1).astype(np.float32)
    arrays["in_rope"] = rope
    args.append(nc.dram_tensor("in_rope", rope.shape, fp32, kind="ExternalInput").ap())
    out = nc.dram_tensor("out_0", (NB, TOK, C1), fp32, kind="ExternalOutput").ap()
    build(nc, *args, out)
    r = run_bass_kernel_spmd(nc, [arrays], core_ids=[0])
    return r.results[0]["out_0"]
```

```python
import concourse.bass as bass
from concourse import mybir
from contextlib import ExitStack

fp32 = mybir.dt.float32
ALU = mybir.AluOpType
ACT = mybir.ActivationFunctionType
AX = mybir.AxisListType

NB, TOK, C1, C2, H = 16, 128, 256, 192, 16
HD = C1 // H
HID = 4 * C1
KT = C1 // 128
C2B = C2 - 128
NG = 4
GH = H // NG
MH = 128 // HD
VW = HD + 1
HM = HID // 128
NP = NB // 2
EPS = 1e-5
EPS_L2 = 1e-12
STEPS_A = NB + 4
STEPS_C = NB + 5
LOADED = 16
QUARTERS = 4


def known(n):
    return isinstance(n, int)


def ok(tile):
    return not known(tile) or 0 <= tile < NB


def wait(eng, sem, count):
    if not known(count) or count > 0:
        eng.wait_ge(sem, count)


def pipeline(eng, step, steps, peeled=6):
    for s in range(peeled):
        step(s // 2, s % 2)
    with eng.Fori(0, (NB - peeled) // 2) as i:
        for j in range(2):
            step(i + peeled // 2, j)
    for s in range(NB, steps):
        step(s // 2, s % 2)


def build(nc, x, ctx, ln1_w, ln1_b, ln2_w, ln2_b, ln3_w, ln3_b, Wq, Wkv, Wproj, bproj, W1, b1, W2, b2,
          norm_w, wq, wkv, wout, rope, halves, out):
    es = ExitStack()
    with es:
        def sb(name, *shape):
            return es.enter_context(nc.sbuf_tensor(name, list(shape), fp32))

        def ps(name):
            return es.enter_context(nc.psum_tensor(name, [128, 512], fp32))

        def sem(name):
            return es.enter_context(nc.semaphore(name))

        ident = sb("ident", 128, 128)
        eps_t = sb("eps_t", 128, 2)
        minus_half = sb("minus_half", 128, 2 * H)
        x_all = sb("x_all", 128, NB, C1)
        ctx_in = sb("ctx_in", 128, 2, C2)
        xn = sb("xn", 128, 2, C1)
        yn = sb("yn", 128, 2, C2)
        inT = sb("inT", 128, 2, 4, TOK)
        qkT = sb("qkT", 128, 2, 4, TOK)
        kmask = sb("kmask", 128, 2, H, TOK)
        vals = sb("vals", 128, 2, H, VW)
        P = sb("P", 128, NG, 512)
        PT = sb("PT", 128, NG, 512)
        oT = sb("oT", 128, 512)
        on = sb("on", 128, C1)
        onT = sb("onT", 128, KT, TOK)
        row_sums_inv = sb("row_sums_inv", 128, H)
        row_max = sb("row_max", 128, NG, GH)
        stats = sb("stats", 128, 2, 12)
        wait_carrier = sb("wait_carrier", 128, 1)
        mean_var = sb("mean_var", 128, 2, 4)
        var_eps = sb("var_eps", 128, 2, 2)
        rstd = sb("rstd", 128, 2, 2)
        Wq_s = sb("Wq_s", 128, KT, C1)
        Wkv_s = sb("Wkv_s", 128, 2, 2 * C1)
        Wproj_s = sb("Wproj_s", 128, KT, C1)
        W1_s = sb("W1_s", 128, KT, HID)
        W2_s = sb("W2_s", 128, HM, C1)
        wq_s = sb("wq_s", 128, KT, C1)
        wkv_s = sb("wkv_s", 128, 2, 2 * C1)
        wout_s = sb("wout_s", 128, KT, C1)
        ln_cols = sb("ln_cols", 128, 7, KT)
        b1_cols = sb("b1_cols", 128, HM)
        b1_all = sb("b1_all", 128, HM)
        ln2b_wide = sb("ln2b_wide", 128, 2, 128)
        qk_bias = sb("qk_bias", 128, 4)
        v_bias = sb("v_bias", 128, C1)
        bproj_row = sb("bproj_row", 128, C1)
        b2_row = sb("b2_row", 128, C1)
        halves_t = sb("halves_t", 128, 2)
        rope_t = sb("rope_t", 128, 2, HD)
        lnT = sb("lnT", 128, KT, 2 * TOK)
        hT = sb("hT", 128, HM, 2 * TOK)
        mean_sq = sb("mean_sq", 128, 2, 1)
        x_sq = sb("x_sq", 128, C1)
        rot_a = sb("rot_a", 128, 2 * C1)
        rot_b = sb("rot_b", 128, 2 * C1)
        rot = sb("rot", 128, 2, 2 * C1)
        rot_sq = sb("rot_sq", 128, 2 * C1)
        norm_sq = sb("norm_sq", 128, 2, 2 * H)
        norm_sq_min = sb("norm_sq_min", 128, 2, 2 * H)
        norm_inv = sb("norm_inv", 128, 2, 2 * H)
        qk_unit = sb("qk_unit", 128, 2 * C1)
        y_out = sb("y_out", 128, 2, C1)

        bank_s = [ps(f"bank_s{n}") for n in range(4)]
        bank_o = ps("bank_o")
        bank_y = ps("bank_y")
        bank_t = ps("bank_t")
        bank_qk = ps("bank_qk")

        in_loaded = [sem(f"in_loaded{j}") for j in range(2)]
        w_att_loaded, w_out_loaded, w_mlp_loaded, w_b1_loaded = sem("w_att"), sem("w_out"), sem("w_mlp"), sem("w_b1")
        const_ready, ident_ready, zero_ready = sem("const_ready"), sem("ident_ready"), sem("zero_ready")
        wide_ready, bias_mm, w_att_ready, w_mlp_ready = sem("wide_ready"), sem("bias_mm"), sem("w_att_ready"), sem("w_mlp_ready")

        def att_sems(n):
            names = ("stats_raw", "stats_ready", "var_ready", "rstd_ready", "norm_done", "in_transposed", "inT_ready",
                     "qk_mm", "qk_ready", "v_mm", "v_ready", "scores", "maxed", "shifted", "exped", "w_transposed",
                     "wT_ready", "av", "oT_ready", "o_back", "recip", "on_ready", "on_transposed", "onT_ready",
                     "proj_mm", "res_ready", "bias_added")
            return {k: sem(f"{n}_{k}") for k in names}

        A, C = att_sems("a"), att_sems("c")
        a_masked, a_masked_pool, c_masked, c_masked_act = (sem(k) for k in ("a_masked", "a_masked_pool", "c_masked", "c_masked_act"))
        c_loaded = [sem(f"c_loaded{j}") for j in range(2)]
        c_stored = [sem(f"c_stored{j}") for j in range(2)]
        c_rope, c_turned, c_rot, c_rot_sq, c_norm_sq, c_norm_min, c_norm_inv, c_unit, c_unit_T = (
            sem(f"c_{k}") for k in ("rope", "turned", "rot", "rot_sq", "norm_sq", "norm_min", "norm_inv", "unit", "unit_T"))
        b_stats_raw, b_stats, b_var, b_rstd, b_norm, b_bias, b_T, b_lnT, b_w1, b_gelu, b_w2, b_x = (
            sem(f"b_{k}") for k in ("stats_raw", "stats", "var", "rstd", "norm", "bias", "T", "lnT", "w1", "gelu", "w2", "x"))

        block = es.enter_context(nc.Block())

        def tile_of(t):
            return x_all[:, bass.ds(t, 1), :].rearrange("p b c -> p (b c)")

        def heads(ap, n=H):
            return ap.rearrange("p (h d) -> p h d", h=n)

        def each(col, n, width):
            return col.unsqueeze(2).broadcast_to([128, n, width])

        def masked(j, quarter, half, keys):
            r = slice(32 * quarter, 32 * quarter + 32)
            first = 2 * quarter + half
            return kmask[r, j, first:H:MH, :], keys[r], halves_t[r, half:half + 1]

        def turned_keys():
            return bank_qk[:, C1:].rearrange("p (a b) -> p a b", a=KT)

        @block.sync
        def _(sp):
            def load_in(t, j, loaded):
                if loaded is in_loaded:
                    sp.dma_start(tile_of(t), x[bass.ds(t, 1)].rearrange("b p c -> p (b c)")).then_inc(loaded[j], LOADED)
                sp.dma_start(ctx_in[:, j, :], ctx[bass.ds(t, 1)].rearrange("b p c -> p (b c)")).then_inc(loaded[j], LOADED)

            for j in range(2):
                load_in(j, j, in_loaded)
            sp.dma_start(Wkv_s[:, 0, :], Wkv[0:128, :]).then_inc(w_att_loaded, LOADED)
            sp.dma_start(Wkv_s[0:C2B, 1, :], Wkv[128:C2, :]).then_inc(w_att_loaded, LOADED)
            sp.dma_start(Wq_s[:, :, :], Wq.rearrange("(t p) n -> p t n", p=128)).then_inc(w_att_loaded, LOADED)
            sp.dma_start(Wproj_s[:, :, :], Wproj.rearrange("(t p) n -> p t n", p=128)).then_inc(w_out_loaded, LOADED)
            sp.dma_start(bproj_row[:, :], bproj.unsqueeze(0).broadcast_to([128, C1])).then_inc(w_out_loaded, LOADED)
            sp.dma_start(b2_row[:, :], b2.unsqueeze(0).broadcast_to([128, C1])).then_inc(w_out_loaded, LOADED)
            sp.dma_start(W1_s[:, :, :], W1.rearrange("(t p) n -> p t n", p=128)).then_inc(w_mlp_loaded, LOADED)
            sp.dma_start(W2_s[:, :, :], W2.rearrange("(t p) n -> p t n", p=128)).then_inc(w_mlp_loaded, LOADED)
            sp.dma_start(wq_s[:, :, :], wq.rearrange("(t p) n -> p t n", p=128)).then_inc(w_mlp_loaded, LOADED)
            sp.dma_start(wkv_s[:, 0, :], wkv[0:128, :]).then_inc(w_mlp_loaded, LOADED)
            sp.dma_start(wkv_s[0:C2B, 1, :], wkv[128:C2, :]).then_inc(w_mlp_loaded, LOADED)
            sp.dma_start(wout_s[:, :, :], wout.rearrange("(t p) n -> p t n", p=128)).then_inc(w_mlp_loaded, LOADED)
            def step_a(p, j):
                s = 2 * p + j
                if ok(s + 2):
                    sp.wait_ge(A["norm_done"], 2 * s + 2)
                    load_in(s + 2, j, in_loaded)

            def step_c(p, j):
                s = 2 * p + j
                if ok(s + 2):
                    sp.wait_ge(C["in_transposed"], s + 1)
                    load_in(s + 2, j, c_loaded)
                if ok(s - 5):
                    sp.wait_ge(C["res_ready"], s - 4)
                    sp.dma_start(out[bass.ds(s - 5, 1)].rearrange("b p c -> p (b c)"), y_out[:, 1 - j, :])\
                        .then_inc(c_stored[1 - j], LOADED)

            def run(step, steps):
                for s in range(6):
                    step(s // 2, s % 2)
                with sp.Fori(0, (NB - 8) // 2) as i:
                    for j in range(2):
                        step(i + 3, j)
                for s in range(NB - 2, steps):
                    step(s // 2, s % 2)

            run(step_a, STEPS_A)
            sp.wait_ge(A["norm_done"], 2 * NB)
            for j in range(2):
                load_in(j, j, c_loaded)
            run(step_c, STEPS_C)
            for j in range(2):
                sp.wait_ge(c_stored[j], NP * LOADED)

        @block.gpsimd
        def _(pool):
            nc.gpsimd.memset(ident[:, :], 0.0).then_inc(ident_ready, 1)
            nc.gpsimd.memset(minus_half[:, :], -0.5).then_inc(const_ready, 1)
            nc.gpsimd.memset(eps_t[:, :], EPS).then_inc(const_ready, 1)
            pool.wait_ge(ident_ready, 1)
            nc.gpsimd.affine_select(out=ident[:, :], in_=ident[:, :], compare_op=ALU.not_equal, fill=1.0, base=0,
                                    pattern=[[-1, 128]], channel_multiplier=1).then_inc(ident_ready, 1)
            for j in range(2):
                nc.gpsimd.memset(kmask[:, j, :, :], 0.0).then_inc(zero_ready, 1)
            nc.gpsimd.memset(vals[:, :, :, :], 1.0).then_inc(zero_ready, 1)

            def step_a(p, j):
                t = 2 * p + j
                if ok(t):
                    pool.wait_ge(A["stats_ready"], 2 * t + 2)
                    nc.gpsimd.tensor_tensor(var_eps[:, j, :], mean_var[:, j, 1:4:2], eps_t[:, :], ALU.add)\
                        .then_inc(A["var_ready"], 1)
                    pool.wait_ge(A["var_ready"], t + 1)
                    nc.gpsimd.tensor_tensor(rstd[:, j, :], var_eps[:, j, :], minus_half[:, 0:2], ALU.pow)\
                        .then_inc(A["rstd_ready"], 1)
                if ok(t - 1):
                    pool.wait_ge(A["qk_ready"], t)
                    wait(pool, A["bias_added"], t)
                    if ok(t):
                        pool.wait_ge(A["rstd_ready"], t + 1)
                    for q in range(QUARTERS):
                        o, keys, ones = masked(1 - j, q, 1, qkT[:, 1 - j, 2:4, :])
                        last = nc.gpsimd.tensor_tensor(o, keys, ones.unsqueeze(2).broadcast_to([32, KT, TOK]), ALU.mult)
                    last.then_inc(a_masked_pool, 1)
                    pool.wait_ge(a_masked_pool, t)
                if ok(t):
                    pool.wait_ge(A["norm_done"], 2 * t + 2)
                    nc.gpsimd.tensor_tensor(tile_of(t), tile_of(t), bproj_row[:, :], ALU.add)\
                        .then_inc(A["bias_added"], 1)

            pool.wait_ge(const_ready, 2)
            pool.wait_ge(w_out_loaded, 3 * LOADED)
            pool.wait_ge(w_b1_loaded, 6 * LOADED)
            pool.wait_ge(zero_ready, 3)
            pipeline(pool, step_a, STEPS_A)

            def norm_b(p):
                pool.wait_ge(b_stats, 2 * p + 2)
                nc.gpsimd.tensor_tensor(var_eps[:, :, 0], mean_var[:, :, 1], eps_t[:, :], ALU.add).then_inc(b_var, 1)
                pool.wait_ge(b_var, p + 1)
                nc.gpsimd.tensor_tensor(rstd[:, :, 0], var_eps[:, :, 0], minus_half[:, 0:2], ALU.pow).then_inc(b_rstd, 1)
                pool.wait_ge(b_norm, 2 * p + 2)
                for j in range(2):
                    nc.gpsimd.tensor_tensor(tile_of(2 * p + j), tile_of(2 * p + j), b2_row[:, :], ALU.add).then_inc(b_bias, 1)

            norm_b(0)
            with pool.Fori(0, NP - 1) as i:
                norm_b(i + 1)

            def step_c(p, j):
                t = 2 * p + j
                if ok(t):
                    pool.wait_ge(C["stats_ready"], t + 1)
                    nc.gpsimd.tensor_tensor(var_eps[:, j, 0:1], mean_sq[:, j, :], eps_t[:, 0:1], ALU.add)\
                        .then_inc(C["var_ready"], 1)
                    pool.wait_ge(C["var_ready"], t + 1)
                    nc.gpsimd.tensor_tensor(rstd[:, j, 0:1], var_eps[:, j, 0:1], minus_half[:, 0:1], ALU.pow)\
                        .then_inc(C["rstd_ready"], 1)
                if ok(t - 1):
                    pool.wait_ge(c_norm_min, t)
                    nc.gpsimd.tensor_tensor(norm_inv[:, 1 - j, :], norm_sq_min[:, 1 - j, :], minus_half[:, :], ALU.pow)\
                        .then_inc(c_norm_inv, 1)

            pipeline(pool, step_c, STEPS_C)

        @block.scalar
        def _(act):
            for n, v in enumerate((ln1_w, ln1_b, ln2_w, ln2_b)):
                if n < 2:
                    act.dma_start(ln_cols[:, n, :], v.rearrange("(t p) -> p t", p=128), allow_slow_non_contiguous=True).then_inc(w_att_loaded, LOADED)
                else:
                    act.dma_start(ln_cols[:, n, 0:1], v[0:128].unsqueeze(1)).then_inc(w_att_loaded, LOADED)
                    act.dma_start(ln_cols[0:C2B, n, 1:2], v[128:C2].unsqueeze(1)).then_inc(w_att_loaded, LOADED)
            for n, v in enumerate((ln3_w, ln3_b, norm_w)):
                act.dma_start(ln_cols[:, 4 + n, :], v.rearrange("(t p) -> p t", p=128), allow_slow_non_contiguous=True).then_inc(w_b1_loaded, LOADED)
            act.dma_start(b1_cols[:, :], b1.rearrange("(t p) -> p t", p=128), allow_slow_non_contiguous=True).then_inc(w_b1_loaded, LOADED)
            act.dma_start(rope_t[:, :, :], rope).then_inc(w_b1_loaded, LOADED)
            act.dma_start(halves_t[:, :], halves).then_inc(w_b1_loaded, LOADED)

            def inputs_T(t, j, S):
                act.wait_ge(S["in_transposed"], t + 1)
                wait(act, S["v_mm"], t - 1)
                nc.scalar.activation(inT[:, j, 0:3, :], bank_t[:, 0:3 * TOK].rearrange("p (a b) -> p a b", a=3), ACT.Copy)\
                    .then_inc(S["inT_ready"], 1)
                nc.scalar.activation(inT[0:C2B, j, 3, :], bank_t[0:C2B, 3 * TOK:], ACT.Copy).then_inc(S["inT_ready"], 1)

            def out_T(f, S):
                act.wait_ge(S["av"], NG * f + NG)
                wait(act, S["o_back"], f)
                nc.scalar.activation(oT[:, :], bank_o[:, :], ACT.Copy).then_inc(S["oT_ready"], 1)

            def on_T(f, S):
                act.wait_ge(S["on_transposed"], f + 1)
                wait(act, S["proj_mm"], f)
                nc.scalar.activation(onT[:, :, :], bank_y[:, 0:C1].rearrange("p (a b) -> p a b", a=KT), ACT.Copy)\
                    .then_inc(S["onT_ready"], 1)

            def step_a(p, j):
                s = 2 * p + j
                a = s - 2

                def exp(g):
                    if ok(a):
                        act.wait_ge(A["shifted"], NG * a + g + 1)
                        nc.scalar.activation(P[:, g, :], P[:, g, :], ACT.Exp, scale=HD ** -0.5).then_inc(A["exped"], 1)

                def weights_T(tile, g):
                    if ok(tile):
                        c = NG * tile + g
                        act.wait_ge(A["w_transposed"], c + 1)
                        wait(act, A["av"], c - 3)
                        nc.scalar.activation(PT[:, g, :], bank_s[2 + g % 2][:, :], ACT.Copy).then_inc(A["wT_ready"], 1)

                if ok(s - 4):
                    on_T(s - 4, A)
                weights_T(a - 1, 2)
                exp(0)
                weights_T(a - 1, 3)
                exp(1)
                if ok(s):
                    inputs_T(s, j, A)
                weights_T(a, 0)
                if ok(a - 1):
                    out_T(a - 1, A)
                exp(2)
                weights_T(a, 1)
                exp(3)

            pipeline(act, step_a, STEPS_A)

            def lnT_b(p, later):
                act.wait_ge(b_T, p + 1)
                if later:
                    act.wait_ge(b_w1, 4 * p)
                nc.scalar.activation(lnT[:, :, :], bank_t[:, :].rearrange("p (a b) -> p a b", a=KT), ACT.Copy)\
                    .then_inc(b_lnT, 1)

            def gelu_b(p, later):
                for u in range(4):
                    act.wait_ge(b_w1, 4 * p + u + 1)
                    if later and u == 0:
                        act.wait_ge(b_w2, 2 * p)
                    for k in range(2):
                        m = 2 * u + k
                        last = nc.scalar.activation(hT[:, m, :], bank_s[u][:, 256 * k:256 * k + 256], ACT.Gelu,
                                                    bias=b1_all[:, m:m + 1])
                    last.then_inc(b_gelu, 1)

            act.wait_ge(w_mlp_ready, 3)
            lnT_b(0, False)
            gelu_b(0, False)
            with act.Fori(0, NP - 1) as i:
                lnT_b(i + 1, True)
                gelu_b(i + 1, True)

            def step_c(p, j):
                s = 2 * p + j
                a = s - 3

                def exp(g):
                    if ok(a):
                        c = NG * a + g
                        act.wait_ge(C["scores"], c + 1)
                        wait(act, C["av"], c - 3)
                        nc.scalar.activation(PT[:, g, :], bank_s[g][:, :], ACT.Exp, scale=HD ** 0.5).then_inc(C["exped"], 1)

                exp(0)
                if ok(s - 1):
                    act.wait_ge(c_rot, s)
                    wait(act, c_norm_sq, s - 1)
                    nc.scalar.activation(rot_sq[:, :], rot[:, 1 - j, :], ACT.Square).then_inc(c_rot_sq, 1)
                if ok(a - 1):
                    out_T(a - 1, C)
                exp(1)
                if ok(s - 2):
                    act.wait_ge(c_turned, s - 1)
                    wait(act, C["scores"], NG * (s - 3))
                    nc.scalar.activation(qkT[:, j, 0:2, :], bank_qk[:, 0:C1].rearrange("p (a b) -> p a b", a=KT), ACT.Copy)\
                        .then_inc(c_unit_T, 1)
                    for q in range(QUARTERS):
                        o, keys, ones = masked(j, q, 1, turned_keys())
                        last = nc.scalar.activation(o, keys, ACT.Copy, scale=ones)
                    last.then_inc(c_masked_act, 1)
                    act.wait_ge(C["v_mm"], s - 1)
                    wait(act, C["av"], NG * (s - 3))
                    nc.scalar.activation(vals[:, j, :, 0:HD], heads(bank_t[:, 0:C1]), ACT.Copy).then_inc(C["v_ready"], 1)
                exp(2)
                if ok(s):
                    inputs_T(s, j, C)
                exp(3)
                if ok(a - 1):
                    on_T(a - 1, C)

            pipeline(act, step_c, STEPS_C)

        @block.tensor
        def _(pe):
            mm = nc.tensor.matmul
            pe.wait_ge(w_att_loaded, 9 * LOADED)
            pe.wait_ge(wide_ready, 2)
            rows = (128, C2B)
            for m in range(KT):
                for k in range(KT):
                    mm(bank_qk[:, m:m + 1], Wq_s[:, k, 128 * m:128 * m + 128], ln_cols[:, 1, k:k + 1],
                       start=k == 0, stop=k == KT - 1)
            for m in range(KT):
                for k, r in enumerate(rows):
                    mm(bank_qk[:, 2 + m:3 + m], Wkv_s[0:r, k, 128 * m:128 * m + 128], ln_cols[0:r, 3, k:k + 1],
                       start=k == 0, stop=k == 1)
            for k, r in enumerate(rows):
                last = mm(bank_t[:, 0:C1], ln2b_wide[0:r, k, :], Wkv_s[0:r, k, C1:], start=k == 0, stop=k == 1)
            last.then_inc(bias_mm, 1)
            pe.wait_ge(w_mlp_loaded, 6 * LOADED)
            pe.wait_ge(w_b1_loaded, 6 * LOADED)
            for m in range(HM):
                for k in range(KT):
                    last = mm(bank_y[:, m:m + 1], W1_s[:, k, 128 * m:128 * m + 128], ln_cols[:, 5, k:k + 1],
                              start=k == 0, stop=k == KT - 1)
            last.then_inc(bias_mm, 1)
            pe.wait_ge(w_att_ready, 4)
            pe.wait_ge(w_mlp_ready, 3)
            pe.wait_ge(ident_ready, 2)

            def inputs_T(j, xs, ys, S):
                for k in range(KT):
                    nc.tensor.transpose(bank_t[:, 128 * k:128 * k + 128], xs[:, j, 128 * k:128 * k + 128], ident[:, :])
                nc.tensor.transpose(bank_t[:, 256:384], ys[:, j, 0:128], ident[:, :])
                nc.tensor.transpose(bank_t[0:C2B, 384:512], ys[:, j, 128:C2], ident[:, :]).then_inc(S["in_transposed"], 1)

            def values(j, w, S):
                for k, r in enumerate(rows):
                    last = mm(bank_t[:, 0:C1], inT[0:r, j, 2 + k, :], w[0:r, k, C1:], start=k == 0, stop=k == 1)
                last.then_inc(S["v_mm"], 1)

            def weighted(a, g, j, S):
                if not ok(a):
                    return
                pe.wait_ge(S["wT_ready"] if S is A else S["exped"], NG * a + g + 1)
                if g == 0:
                    pe.wait_ge(S["v_ready"], a + 1)
                    wait(pe, S["oT_ready"], a)
                for r in range(GH):
                    last = mm(bank_o[32 * r:32 * r + VW, 128 * g:128 * g + 128], vals[:, j, GH * g + r, :],
                              PT[:, g, 128 * r:128 * r + 128], start=True, stop=True)
                last.then_inc(S["av"], 1)

            def back(f, S):
                if ok(f):
                    pe.wait_ge(S["oT_ready"], f + 1)
                    wait(pe, S["res_ready"], f)
                    for g in range(NG):
                        last = nc.tensor.transpose(bank_y[:, 128 * g:128 * g + 128], oT[:, 128 * g:128 * g + 128], ident[:, :])
                    last.then_inc(S["o_back"], 1)

            def normed_T(f, S):
                if ok(f):
                    pe.wait_ge(S["on_ready"], f + 1)
                    for k in range(KT):
                        last = nc.tensor.transpose(bank_y[:, 128 * k:128 * k + 128], on[:, 128 * k:128 * k + 128], ident[:, :])
                    last.then_inc(S["on_transposed"], 1)

            def project(f, w, S):
                if ok(f):
                    pe.wait_ge(S["onT_ready"], f + 1)
                    for k in range(KT):
                        last = mm(bank_y[:, 0:C1], onT[:, k, :], w[:, k, :], start=k == 0, stop=k == KT - 1)
                    last.then_inc(S["proj_mm"], 1)

            def step_a(p, j):
                s = 2 * p + j
                a, i = s - 2, 1 - j

                def score(g):
                    if ok(a):
                        c = NG * a + g
                        if g == 0:
                            pe.wait_ge(A["qk_ready"], a + 1)
                            pe.wait_ge(a_masked, a + 1)
                            pe.wait_ge(a_masked_pool, a + 1)
                        wait(pe, A["shifted"], c - 1)
                        mm(bank_s[g % 2][:, :], qkT[:, j, g // 2, :], kmask[:, j, GH * g:GH * g + GH, :],
                           start=True, stop=True).then_inc(A["scores"], 1)

                def weights_T(tile, g):
                    if ok(tile):
                        c = NG * tile + g
                        pe.wait_ge(A["exped"], c + 1)
                        wait(pe, A["wT_ready"], c - 1)
                        for r in range(GH):
                            last = nc.tensor.transpose(bank_s[2 + g % 2][:, 128 * r:128 * r + 128],
                                                       P[:, g, 128 * r:128 * r + 128], ident[:, :])
                        last.then_inc(A["w_transposed"], 1)

                score(0)
                normed_T(s - 4, A)
                weights_T(a - 1, 2)
                if ok(s - 1):
                    pe.wait_ge(A["inT_ready"], 2 * s)
                    wait(pe, A["qk_ready"], s - 1)
                    for m in range(KT):
                        for k in range(KT):
                            mm(bank_qk[:, 128 * m:128 * m + 128], Wq_s[:, k, 128 * m:128 * m + 128], inT[:, i, k, :],
                               start=k == 0, stop=k == KT - 1)
                weighted(a - 1, 1, i, A)
                score(1)
                if ok(s - 1):
                    for m in range(KT):
                        for k, r in enumerate(rows):
                            last = mm(bank_qk[:, 256 + 128 * m:384 + 128 * m], Wkv_s[0:r, k, 128 * m:128 * m + 128],
                                      inT[0:r, i, 2 + k, :], start=k == 0, stop=k == 1)
                    last.then_inc(A["qk_mm"], 1)
                weights_T(a - 1, 3)
                project(s - 4, Wproj_s, A)
                weighted(a - 1, 2, i, A)
                score(2)
                if ok(s):
                    pe.wait_ge(A["norm_done"], 2 * s + 2)
                    wait(pe, A["v_ready"], s - 1)
                    inputs_T(j, xn, yn, A)
                weights_T(a, 0)
                weighted(a - 1, 3, i, A)
                score(3)
                weights_T(a, 1)
                if ok(s - 1):
                    wait(pe, A["inT_ready"], 2 * s + 2 if ok(s) else 2 * s)
                    values(i, Wkv_s, A)
                back(a - 1, A)
                weighted(a, 0, j, A)

            pe.wait_ge(w_out_loaded, 3 * LOADED)
            pipeline(pe, step_a, STEPS_A)

            pe.wait_ge(A["v_ready"], NB)
            pe.wait_ge(A["shifted"], NG * NB)
            pe.wait_ge(A["wT_ready"], NG * NB)
            pe.wait_ge(A["oT_ready"], NB)
            pe.wait_ge(A["res_ready"], NB)

            def turn_b(p):
                pe.wait_ge(b_norm, 2 * p + 2)
                for k in range(KT):
                    for j in range(2):
                        n = 2 * k + j
                        last = nc.tensor.transpose(bank_t[:, 128 * n:128 * n + 128], xn[:, j, 128 * k:128 * k + 128], ident[:, :])
                last.then_inc(b_T, 1)

            def up_b(p, later):
                pe.wait_ge(b_lnT, p + 1)
                for u in range(4):
                    if later:
                        pe.wait_ge(b_gelu, 4 * p + u - 3)
                    for m in (2 * u, 2 * u + 1):
                        for k in range(KT):
                            last = mm(bank_s[u][:, 256 * (m % 2):256 * (m % 2) + 256], W1_s[:, k, 128 * m:128 * m + 128],
                                      lnT[:, k, :], start=k == 0, stop=k == KT - 1)
                    last.then_inc(b_w1, 1)

            def down_b(p, later):
                for j, bank in enumerate((bank_o, bank_y)):
                    if later:
                        pe.wait_ge(b_x, 2 * p + j - 1)
                    for m in range(HM):
                        if j == 0 and m % 2 == 0:
                            pe.wait_ge(b_gelu, 4 * p + m // 2 + 1)
                        last = mm(bank[:, 0:C1], hT[:, m, 128 * j:128 * j + 128], W2_s[:, m, :], start=m == 0, stop=m == HM - 1)
                    last.then_inc(b_w2, 1)

            turn_b(0)
            up_b(0, False)
            turn_b(1)
            down_b(0, False)
            with pe.Fori(0, NP - 2) as i:
                up_b(i + 1, True)
                turn_b(i + 2)
                down_b(i + 1, True)
            up_b(NP - 1, True)
            down_b(NP - 1, True)

            pe.wait_ge(b_x, NB)
            pe.wait_ge(b_gelu, 4 * NP)

            def step_c(p, j):
                s = 2 * p + j
                a, i = s - 3, 1 - j

                def score(g):
                    if ok(a):
                        c = NG * a + g
                        if g == 0:
                            pe.wait_ge(c_unit_T, a + 1)
                            pe.wait_ge(c_masked, a + 1)
                            pe.wait_ge(c_masked_act, a + 1)
                        wait(pe, C["exped"], c - 3)
                        for r in range(GH):
                            last = mm(bank_s[g][:, 128 * r:128 * r + 128], kmask[:, i, GH * g + r, :], qkT[:, i, g // 2, :],
                                      start=True, stop=True)
                        last.then_inc(C["scores"], 1)

                if ok(s - 1):
                    pe.wait_ge(C["inT_ready"], 2 * s)
                    wait(pe, c_unit_T, s - 2)
                    wait(pe, c_masked, s - 2)
                    wait(pe, c_masked_act, s - 2)
                    for k in range(KT):
                        mm(bank_qk[:, 0:C1], inT[:, i, k, :], wq_s[:, k, :], start=k == 0, stop=k == KT - 1)
                    for k, r in enumerate(rows):
                        last = mm(bank_qk[:, C1:], inT[0:r, i, 2 + k, :], wkv_s[0:r, k, 0:C1], start=k == 0, stop=k == 1)
                    last.then_inc(C["qk_mm"], 1)
                score(0)
                project(s - 5, wout_s, C)
                weighted(a - 1, 3, j, C)
                score(1)
                if ok(s - 2):
                    pe.wait_ge(c_unit, s - 1)
                    wait(pe, c_rope, 2 * s if ok(s - 1) else 2 * s - 2)
                    for n in range(4):
                        last = nc.tensor.transpose(bank_qk[:, 128 * n:128 * n + 128], qk_unit[:, 128 * n:128 * n + 128], ident[:, :])
                    last.then_inc(c_turned, 1)
                weighted(a, 0, i, C)
                back(a - 1, C)
                if ok(s - 2):
                    wait(pe, C["inT_ready"], 2 * s if ok(s - 1) else 2 * s - 2)
                    values(j, wkv_s, C)
                score(2)
                weighted(a, 1, i, C)
                if ok(s):
                    pe.wait_ge(C["norm_done"], s + 1)
                    pe.wait_ge(c_loaded[j], LOADED * (p + 1))
                    wait(pe, C["v_ready"], s - 1)
                    inputs_T(j, xn, ctx_in, C)
                score(3)
                normed_T(a - 1, C)
                weighted(a, 2, i, C)

            pipeline(pe, step_c, STEPS_C)

        @block.vector
        def _(dve):
            v = nc.vector
            v.memset(bank_o[:, :], 0.0).then_inc(wide_ready, 1)
            dve.wait_ge(w_att_loaded, 9 * LOADED)
            for k, r in enumerate((128, C2B)):
                last = v.tensor_copy(ln2b_wide[0:r, k, :], ln_cols[0:r, 3, k:k + 1].broadcast_to([r, 128]))
            last.then_inc(wide_ready, 1)
            dve.wait_ge(bias_mm, 1)
            v.tensor_copy(qk_bias[:, :], bank_qk[:, 0:4]).then_inc(w_att_ready, 1)
            v.tensor_copy(v_bias[:, :], bank_t[:, 0:C1]).then_inc(w_att_ready, 1)
            for k in range(KT):
                last = v.tensor_scalar(Wq_s[:, k, :], Wq_s[:, k, :], ln_cols[:, 0, k:k + 1], None, ALU.mult)
            last.then_inc(w_att_ready, 1)
            for k, r in enumerate((128, C2B)):
                last = v.tensor_scalar(Wkv_s[0:r, k, :], Wkv_s[0:r, k, :], ln_cols[0:r, 2, k:k + 1], None, ALU.mult)
            last.then_inc(w_att_ready, 1)
            dve.wait_ge(bias_mm, 2)
            v.tensor_tensor(b1_all[:, :], bank_y[:, 0:HM], b1_cols[:, :], ALU.add).then_inc(w_mlp_ready, 1)
            for k in range(KT):
                last = v.tensor_scalar(W1_s[:, k, :], W1_s[:, k, :], ln_cols[:, 4, k:k + 1], None, ALU.mult)
            last.then_inc(w_mlp_ready, 1)
            for k in range(KT):
                last = v.tensor_scalar(wq_s[:, k, :], wq_s[:, k, :], ln_cols[:, 6, k:k + 1], None, ALU.mult)
            last.then_inc(w_mlp_ready, 1)

            def values(t, j, S):
                dve.wait_ge(S["v_mm"], t + 1)
                wait(dve, S["av"], NG * (t - 1))
                v.tensor_tensor(vals[:, j, :, 0:HD], heads(bank_t[:, 0:C1]), heads(v_bias[:, :]), ALU.add)\
                    .then_inc(S["v_ready"], 1)

            def normalise_heads(f, S):
                o = bank_y[:, :].rearrange("p (h d) -> p h d", h=H)
                dve.wait_ge(S["o_back"], f + 1)
                v.reciprocal(row_sums_inv[:, :], o[:, :, HD]).then_inc(S["recip"], 1)
                dve.wait_ge(S["recip"], f + 1)
                wait(dve, S["on_transposed"], f)
                v.tensor_tensor(heads(on[:, :]), o[:, :, 0:HD], each(row_sums_inv[:, :], H, HD), ALU.mult)\
                    .then_inc(S["on_ready"], 1)

            def step_a(p, j):
                s = 2 * p + j
                a, i = s - 2, 1 - j

                def shift(g):
                    if ok(a):
                        c = NG * a + g
                        sc = heads(bank_s[g % 2][:, :], GH)
                        dve.wait_ge(A["scores"], c + 1)
                        v.tensor_reduce(row_max[:, g, :], sc, AX.X, ALU.max).then_inc(A["maxed"], 1)
                        dve.wait_ge(A["maxed"], c + 1)
                        wait(dve, A["w_transposed"], c - 3)
                        v.tensor_tensor(heads(P[:, g, :], GH), sc, each(row_max[:, g, :], GH, TOK), ALU.subtract)\
                            .then_inc(A["shifted"], 1)

                if ok(s):
                    dve.wait_ge(in_loaded[j], 2 * LOADED * (p + 1))
                    v.bn_stats(stats[:, j, 0:6], tile_of(s)).then_inc(A["stats_raw"], 1)
                    v.bn_stats(stats[:, j, 6:12], ctx_in[:, j, :]).then_inc(A["stats_raw"], 1)
                    dve.wait_ge(A["stats_raw"], 2 * s + 2)
                    v.tensor_copy(wait_carrier[:, :], stats[:, j, 0:1])
                    v.bn_aggr(mean_var[:, j, 0:2], stats[:, j, 0:6]).then_inc(A["stats_ready"], 1)
                    v.bn_aggr(mean_var[:, j, 2:4], stats[:, j, 6:12]).then_inc(A["stats_ready"], 1)
                shift(0)
                shift(1)
                if ok(s):
                    dve.wait_ge(A["stats_ready"], 2 * s + 2)
                    dve.wait_ge(A["rstd_ready"], s + 1)
                    wait(dve, A["in_transposed"], s - 1)
                    v.tensor_scalar(xn[:, j, :], tile_of(s), mean_var[:, j, 0:1], rstd[:, j, 0:1],
                                    ALU.subtract, ALU.mult).then_inc(A["norm_done"], 1)
                    v.tensor_scalar(yn[:, j, :], ctx_in[:, j, :], mean_var[:, j, 2:3], rstd[:, j, 1:2],
                                    ALU.subtract, ALU.mult).then_inc(A["norm_done"], 1)
                if ok(s - 1):
                    dve.wait_ge(A["qk_mm"], s)
                    wait(dve, A["scores"], NG * (s - 2))
                    wait(dve, a_masked_pool, s - 2)
                    v.tensor_tensor(qkT[:, i, :, :], bank_qk[:, :].rearrange("p (a b) -> p a b", a=4),
                                    each(qk_bias[:, :], 4, TOK), ALU.add).then_inc(A["qk_ready"], 1)
                    dve.wait_ge(A["qk_ready"], s)
                    for q in range(QUARTERS):
                        o, keys, ones = masked(i, q, 0, qkT[:, i, 2:4, :])
                        last = v.tensor_scalar(o, keys, ones, None, ALU.mult)
                    last.then_inc(a_masked, 1)
                shift(2)
                if ok(s - 4):
                    dve.wait_ge(A["proj_mm"], s - 3)
                    dve.wait_ge(A["bias_added"], s - 3)
                    v.tensor_tensor(tile_of(s - 4), tile_of(s - 4), bank_y[:, 0:C1], ALU.add).then_inc(A["res_ready"], 1)
                shift(3)
                if ok(s - 1):
                    values(s - 1, i, A)
                if ok(a - 1):
                    normalise_heads(a - 1, A)

            dve.wait_ge(w_att_ready, 4)
            dve.wait_ge(zero_ready, 3)
            pipeline(dve, step_a, STEPS_A)

            dve.wait_ge(A["res_ready"], NB)
            dve.wait_ge(A["in_transposed"], NB)

            def norm_b(p, later):
                for j in range(2):
                    v.bn_stats(stats[:, j, 0:6], tile_of(2 * p + j)).then_inc(b_stats_raw, 1)
                dve.wait_ge(b_stats_raw, 2 * p + 2)
                v.tensor_copy(wait_carrier[:, :], stats[:, 0, 0:1])
                for j in range(2):
                    v.bn_aggr(mean_var[:, j, 0:2], stats[:, j, 0:6]).then_inc(b_stats, 1)
                dve.wait_ge(b_stats, 2 * p + 2)
                dve.wait_ge(b_rstd, p + 1)
                if later:
                    dve.wait_ge(b_T, p)
                for j in range(2):
                    v.tensor_scalar(xn[:, j, :], tile_of(2 * p + j), mean_var[:, j, 0:1], rstd[:, j, 0:1],
                                    ALU.subtract, ALU.mult).then_inc(b_norm, 1)

            def res_b(p):
                for j, bank in enumerate((bank_o, bank_y)):
                    dve.wait_ge(b_w2, 2 * p + j + 1)
                    dve.wait_ge(b_bias, 2 * p + j + 1)
                    v.tensor_tensor(tile_of(2 * p + j), tile_of(2 * p + j), bank[:, 0:C1], ALU.add).then_inc(b_x, 1)

            norm_b(0, False)
            with dve.Fori(0, NP - 1) as i:
                norm_b(i + 1, True)
                res_b(i)
            res_b(NP - 1)

            dve.wait_ge(b_x, NB)
            dve.wait_ge(b_T, NP)

            def step_c(p, j):
                s = 2 * p + j
                i = 1 - j
                if ok(s):
                    v.scalar_tensor_tensor(x_sq[:, :], tile_of(s), 1.0 / C1, tile_of(s), ALU.mult, ALU.mult,
                                           accum_out=mean_sq[:, j, :]).then_inc(C["stats_ready"], 1)
                if ok(s - 1):
                    dve.wait_ge(C["qk_mm"], s)
                    cos = rope_t[:, 0, :].unsqueeze(1).broadcast_to([128, 2 * H, HD])
                    sin = rope_t[:, 1, :].rearrange("p (s d) -> p s d", s=2).unsqueeze(1).broadcast_to([128, 2 * H, 2, HD // 2])
                    swapped = bank_qk[:, :].rearrange("p (h s d) -> p h s d", s=2, d=HD // 2)[:, :, ::-1, :]
                    v.tensor_tensor(heads(rot_a[:, :], 2 * H), heads(bank_qk[:, :], 2 * H), cos, ALU.mult).then_inc(c_rope, 1)
                    v.tensor_tensor(rot_b[:, :].rearrange("p (h s d) -> p h s d", s=2, d=HD // 2), swapped, sin, ALU.mult)\
                        .then_inc(c_rope, 1)
                    dve.wait_ge(c_rope, 2 * s)
                    v.tensor_tensor(rot[:, i, :], rot_a[:, :], rot_b[:, :], ALU.add).then_inc(c_rot, 1)
                if ok(s - 2):
                    dve.wait_ge(c_norm_inv, s - 1)
                    wait(dve, c_turned, s - 2)
                    v.tensor_tensor(heads(qk_unit[:, :], 2 * H), heads(rot[:, j, :], 2 * H),
                                    each(norm_inv[:, j, :], 2 * H, HD), ALU.mult).then_inc(c_unit, 1)
                if ok(s - 5):
                    dve.wait_ge(C["proj_mm"], s - 4)
                    wait(dve, c_stored[i], LOADED * (p - 2 if j else p - 3))
                    v.tensor_tensor(y_out[:, i, :], tile_of(s - 5), bank_y[:, 0:C1], ALU.add).then_inc(C["res_ready"], 1)
                if ok(s - 1):
                    dve.wait_ge(c_rot_sq, s)
                    v.tensor_reduce(norm_sq[:, i, :], heads(rot_sq[:, :], 2 * H), AX.X, ALU.add).then_inc(c_norm_sq, 1)
                    dve.wait_ge(c_norm_sq, s)
                    v.tensor_scalar(norm_sq_min[:, i, :], norm_sq[:, i, :], EPS_L2 ** 2, None, ALU.max).then_inc(c_norm_min, 1)
                if ok(s):
                    dve.wait_ge(C["stats_ready"], s + 1)
                    dve.wait_ge(C["rstd_ready"], s + 1)
                    wait(dve, C["in_transposed"], s - 1)
                    v.tensor_scalar(xn[:, j, :], tile_of(s), rstd[:, j, 0:1], None, ALU.mult).then_inc(C["norm_done"], 1)
                if ok(s - 4):
                    normalise_heads(s - 4, C)
                if ok(s - 2):
                    dve.wait_ge(c_masked_act, s - 1)
                    wait(dve, C["scores"], NG * (s - 3))
                    for q in range(QUARTERS):
                        o, keys, ones = masked(j, q, 0, turned_keys())
                        last = v.tensor_scalar(o, keys, ones, None, ALU.mult)
                    last.then_inc(c_masked, 1)

            pipeline(dve, step_c, STEPS_C, peeled=8)


_INS = ['x', 'ctx_768', 'L0_xattn_ln1_w', 'L0_xattn_ln1_b', 'L0_xattn_ln2_w', 'L0_xattn_ln2_b', 'L0_xattn_ln3_w',
        'L0_xattn_ln3_b', 'L0_xattn_Wq', 'L0_xattn_Wkv', 'L0_xattn_Wproj', 'L0_xattn_bproj', 'L0_xattn_W1',
        'L0_xattn_b1', 'L0_xattn_W2', 'L0_xattn_b2', 'L1_xattn_norm_w', 'L1_xattn_wq', 'L1_xattn_wkv', 'L1_xattn_wout']


def kernel(**inputs):
    import numpy as np
    import concourse.bacc as bacc
    from concourse.bass_utils import run_bass_kernel_spmd

    nc = bacc.Bacc("TRN2", target_bir_lowering=False, num_devices=1)
    arrays, args = {}, []
    for name in _INS:
        a = np.ascontiguousarray(inputs[name])
        arrays[f"in_{name}"] = a
        args.append(nc.dram_tensor(f"in_{name}", a.shape, mybir.dt.from_np(a.dtype), kind="ExternalInput").ap())
    inv_freq = 1.0 / 10000.0 ** (np.arange(0, HD, 2, dtype=np.float32) / HD)
    angles = np.einsum('i,j->ij', np.arange(TOK, dtype=np.float32), inv_freq)
    rope = np.stack([np.cos(np.concatenate([angles, angles], -1)),
                     np.concatenate([-np.sin(angles), np.sin(angles)], -1)], 1).astype(np.float32)
    arrays["in_rope"] = rope
    args.append(nc.dram_tensor("in_rope", rope.shape, fp32, kind="ExternalInput").ap())
    halves = np.repeat(np.tile(np.eye(2, dtype=np.float32), (4, 1)), HD, 0)
    arrays["in_halves"] = halves
    args.append(nc.dram_tensor("in_halves", halves.shape, fp32, kind="ExternalInput").ap())
    out = nc.dram_tensor("out_0", (NB, TOK, C1), fp32, kind="ExternalOutput").ap()
    build(nc, *args, out)
    r = run_bass_kernel_spmd(nc, [arrays], core_ids=[0])
    return r.results[0]["out_0"]
```

```python
import concourse.bass as bass
from concourse import mybir
from contextlib import ExitStack

fp32 = mybir.dt.float32
fp32r = mybir.dt.float32r
ALU = mybir.AluOpType
ACT = mybir.ActivationFunctionType
AX = mybir.AxisListType

NB, TOK, C1, C2, H = 16, 128, 256, 192, 16
HD = C1 // H
HID = 4 * C1
KT = C1 // 128
C2B = C2 - 128
NG = 4
GH = H // NG
MH = 128 // HD
VW = HD + 1
HM = HID // 128
NP = NB // 2
EPS = 1e-5
EPS_L2 = 1e-12
STEPS_A = NB + 4
STEPS_C = NB + 5
LOADED = 16
HI_LO = ((0, 0), (0, 1), (1, 0))
QUARTERS = 4


def known(n):
    return isinstance(n, int)


def ok(tile):
    return not known(tile) or 0 <= tile < NB


def wait(eng, sem, count):
    if not known(count) or count > 0:
        eng.wait_ge(sem, count)


def at(step, *numbers):
    for s in numbers:
        step(s // 2, s % 2)


def pipeline(eng, step, first, stop, peeled=6, behind=NB):
    at(step, *range(first, peeled))
    with eng.Fori(0, (behind - peeled) // 2) as i:
        for j in range(2):
            step(i + peeled // 2, j)
    at(step, *range(behind, stop))


def build(nc, x, ctx, ln1_w, ln1_b, ln2_w, ln2_b, ln3_w, ln3_b, Wq, Wkv, Wproj, bproj, W1, b1, W2, b2,
          norm_w, wq, wkv, wout, rope, halves, out):
    es = ExitStack()
    with es:
        def sb(name, *shape, dtype=fp32):
            return es.enter_context(nc.sbuf_tensor(name, list(shape), dtype))

        def ps(name):
            return es.enter_context(nc.psum_tensor(name, [128, 512], fp32))

        def sem(name):
            return es.enter_context(nc.semaphore(name))

        ident = sb("ident", 128, 128)
        eps_t = sb("eps_t", 128, 2)
        minus_half = sb("minus_half", 128, 2 * H)
        x_all = sb("x_all", 128, NB, C1)
        ctx_in = sb("ctx_in", 128, 2, C2)
        xn = sb("xn", 128, 2, C1)
        yn = sb("yn", 128, 2, C2)
        inT = sb("inT", 128, 2, 4, TOK)
        qkT = sb("qkT", 128, 2, 4, TOK)
        qkT_r = sb("qkT_r", 128, 2, 2, 4, TOK, dtype=fp32r)
        solo = sb("solo", 128, 2, 2, H, TOK, dtype=fp32r)
        zero = sb("zero", 128, 1)
        vals = sb("vals", 128, 2, H, VW)
        P = sb("P", 128, NG, 512)
        rot_a, rot_b, rot_sq, qk_unit = (P[:, g, :] for g in range(NG))
        PT = sb("PT", 128, NG, 512)
        oT = sb("oT", 128, 512)
        on = sb("on", 128, C1)
        onT = sb("onT", 128, KT, TOK)
        row_sums_inv = sb("row_sums_inv", 128, H)
        row_max = sb("row_max", 128, NG, GH)
        stats = sb("stats", 128, 2, 12)
        wait_carrier = sb("wait_carrier", 128, 1)
        mean_var = sb("mean_var", 128, 2, 4)
        var_eps = sb("var_eps", 128, 2, 2)
        rstd = sb("rstd", 128, 2, 2)
        Wq_s = sb("Wq_s", 128, KT, C1)
        Wkv_s = sb("Wkv_s", 128, 2, 2 * C1)
        Wq_n = sb("Wq_n", 128, KT, C1)
        Wkv_n = sb("Wkv_n", 128, 2, 2 * C1)
        Wproj_s = sb("Wproj_s", 128, KT, C1)
        W1_s = sb("W1_s", 128, KT, HID)
        W2_s = sb("W2_s", 128, HM, C1)
        wq_s, wkv_s = Wq_s, Wkv_s
        y_out = Wq_s
        wout_s = sb("wout_s", 128, KT, C1)
        wq_r = sb("wq_r", 128, 2, KT, C1, dtype=fp32r)
        wkv_r = sb("wkv_r", 128, 2, 2, 2 * C1, dtype=fp32r)
        wout_r = sb("wout_r", 128, 2, KT, C1, dtype=fp32r)
        inT_r = sb("inT_r", 128, 2, 2, 4, TOK, dtype=fp32r)
        onT_r = sb("onT_r", 128, 2, KT, TOK, dtype=fp32r)
        ln_cols = sb("ln_cols", 128, 7, KT)
        b1_cols = sb("b1_cols", 128, HM)
        b1_all = sb("b1_all", 128, HM)
        ln2b_wide = sb("ln2b_wide", 128, 2, 128)
        qk_bias = sb("qk_bias", 128, 4)
        v_bias = sb("v_bias", 128, C1)
        bproj_row = sb("bproj_row", 128, C1)
        b2_row = sb("b2_row", 128, C1)
        halves_t = sb("halves_t", 128, 2)
        rope_t = sb("rope_t", 128, 2, HD)
        W1_hi, W1_lo = (sb(n, 128, KT, HID, dtype=fp32r) for n in ("W1_hi", "W1_lo"))
        W2_hi, W2_lo = (sb(n, 128, HM, C1, dtype=fp32r) for n in ("W2_hi", "W2_lo"))
        lnT_hi, lnT_lo = (sb(n, 128, KT, 2 * TOK, dtype=fp32r) for n in ("lnT_hi", "lnT_lo"))
        hT_hi, hT_lo = (sb(n, 128, HM, 2 * TOK, dtype=fp32r) for n in ("hT_hi", "hT_lo"))
        hT = W1_s[:, :, :].rearrange("p k (m n) -> p (k m) n", n=2 * TOK)
        mean_sq = sb("mean_sq", 128, 2, 1)
        x_sq = W2_s[:, HM - 1, :]
        rot = W2_s[:, 0:4, :].rearrange("p (j k) n -> p j (k n)", j=2)
        norm_sq = sb("norm_sq", 128, 2, 2 * H)
        norm_sq_min = sb("norm_sq_min", 128, 2, 2 * H)
        norm_inv = sb("norm_inv", 128, 2, 2 * H)

        bank_s = [ps(f"bank_s{n}") for n in range(4)]
        bank_o = ps("bank_o")
        bank_y = ps("bank_y")
        bank_t = ps("bank_t")
        bank_qk = ps("bank_qk")

        in_loaded = [sem(f"in_loaded{j}") for j in range(2)]
        w_att_loaded, w_out_loaded, w_mlp_loaded, w_b1_loaded = sem("w_att"), sem("w_out"), sem("w_mlp"), sem("w_b1")
        const_ready, ident_ready, zero_ready, rows_zeroed = (sem(k) for k in ("const", "ident", "zero", "rows_zeroed"))
        wide_ready, bias_mm, w_att_ready, w_mlp_ready = sem("wide_ready"), sem("bias_mm"), sem("w_att_ready"), sem("w_mlp_ready")
        w1_hi_done, w1_lo_done, w2_hi_done, w2_lo_done = (sem(k) for k in ("w1_hi_done", "w1_lo_done", "w2_hi_done", "w2_lo_done"))

        def att_sems(n):
            names = ("stats_raw", "stats_ready", "var_ready", "rstd_ready", "norm_done", "in_transposed", "inT_ready",
                     "qk_mm", "qk_ready", "v_mm", "v_ready", "scores", "maxed", "shifted", "exped", "w_transposed",
                     "wT_ready", "av", "oT_ready", "o_back", "recip", "on_ready", "on_transposed", "onT_ready",
                     "proj_mm", "res_ready", "bias_added")
            return {k: sem(f"{n}_{k}") for k in names}

        A, C = att_sems("a"), att_sems("c")
        a_alone_act, a_alone_pool, c_alone_act, c_alone_dve = (
            sem(k) for k in ("a_alone_act", "a_alone_pool", "c_alone_act", "c_alone_dve"))
        a_qk_hi, a_qk_lo = sem("a_qk_hi"), sem("a_qk_lo")
        c_inT_lo, c_onT_lo, wc_hi, wc_lo = (sem(k) for k in ("c_inT_lo", "c_onT_lo", "wc_hi", "wc_lo"))
        c_loaded = [sem(f"c_loaded{j}") for j in range(2)]
        c_stored = [sem(f"c_stored{j}") for j in range(2)]
        c_rope, c_turned, c_rot, c_rot_sq, c_norm_sq, c_norm_min, c_norm_inv, c_unit, c_unit_hi, c_unit_lo = (
            sem(f"c_{k}") for k in ("rope", "turned", "rot", "rot_sq", "norm_sq", "norm_min", "norm_inv", "unit", "unit_hi", "unit_lo"))
        b_stats_raw, b_stats, b_var, b_rstd, b_norm, b_bias, b_T, b_lnT_hi, b_lnT_lo, b_w1, b_gelu, b_hT_hi, b_hT_lo, b_w2, b_x = (
            sem(f"b_{k}") for k in ("stats_raw", "stats", "var", "rstd", "norm", "bias", "T", "lnT_hi", "lnT_lo", "w1", "gelu",
                                    "hT_hi", "hT_lo", "w2", "x"))

        block = es.enter_context(nc.Block())

        def tile_of(t):
            return x_all[:, bass.ds(t, 1), :].rearrange("p b c -> p (b c)")

        def heads(ap, n=H):
            return ap.rearrange("p (h d) -> p h d", h=n)

        def each(col, n, width):
            return col.unsqueeze(2).broadcast_to([128, n, width])

        def alone(j, quarter, half, first_tile):
            r = slice(32 * quarter, 32 * quarter + 32)
            head = 2 * quarter + half
            return (solo[r, j, :, head:H:MH, :], qkT_r[r, j, :, first_tile:first_tile + KT, :].bitcast(fp32),
                    halves_t[r, half:half + 1])

        bias_parts = {2: range(0, 3), 3: range(3, 6), 4: range(6, HM)}

        def part(u):
            return slice(2 * u, 2 * u + 2)

        def w1_part(w, u):
            return w[:, u % 2, HID // 2 * (u // 2):HID // 2 * (u // 2 + 1)]

        @block.sync
        def _(sp):
            def load_in(t, j, loaded):
                if loaded is in_loaded:
                    sp.dma_start(tile_of(t), x[bass.ds(t, 1)].rearrange("b p c -> p (b c)")).then_inc(loaded[j], LOADED)
                sp.dma_start(ctx_in[:, j, :], ctx[bass.ds(t, 1)].rearrange("b p c -> p (b c)")).then_inc(loaded[j], LOADED)

            load_in(0, 0, in_loaded)
            sp.dma_start(Wkv_s[:, 0, :], Wkv[0:128, :]).then_inc(w_att_loaded, LOADED)
            sp.dma_start(Wkv_s[0:C2B, 1, :], Wkv[128:C2, :]).then_inc(w_att_loaded, LOADED)
            sp.dma_start(Wq_s[:, :, :], Wq.rearrange("(t p) n -> p t n", p=128)).then_inc(w_att_loaded, LOADED)
            sp.dma_start(halves_t[:, :], halves).then_inc(w_b1_loaded, LOADED)
            load_in(1, 1, in_loaded)
            sp.dma_start(rope_t[:, :, :], rope).then_inc(w_b1_loaded, LOADED)
            for n, w in enumerate((ln3_w, ln3_b, norm_w)):
                sp.dma_start(ln_cols[:, 4 + n, :], w.rearrange("(t p) -> p t", p=128), allow_slow_non_contiguous=True).then_inc(w_b1_loaded, LOADED)
            sp.dma_start(b1_cols[:, :], b1.rearrange("(t p) -> p t", p=128), allow_slow_non_contiguous=True).then_inc(w_b1_loaded, LOADED)
            sp.dma_start(Wproj_s[:, :, :], Wproj.rearrange("(t p) n -> p t n", p=128)).then_inc(w_out_loaded, LOADED)
            sp.dma_start(bproj_row[:, :], bproj.unsqueeze(0).broadcast_to([128, C1])).then_inc(w_out_loaded, LOADED)
            sp.dma_start(b2_row[:, :], b2.unsqueeze(0).broadcast_to([128, C1])).then_inc(w_out_loaded, LOADED)
            sp.dma_start(W1_s[:, :, :], W1.rearrange("(t p) n -> p t n", p=128)).then_inc(w_mlp_loaded, LOADED)
            sp.dma_start(W2_s[:, :, :], W2.rearrange("(t p) n -> p t n", p=128)).then_inc(w_mlp_loaded, LOADED)
            sp.dma_start(wout_s[:, :, :], wout.rearrange("(t p) n -> p t n", p=128)).then_inc(w_mlp_loaded, LOADED)
            sp.wait_ge(w_att_ready, 4)
            sp.dma_start(wq_s[:, :, :], wq.rearrange("(t p) n -> p t n", p=128)).then_inc(w_mlp_loaded, LOADED)
            sp.dma_start(wkv_s[:, 0, :], wkv[0:128, :]).then_inc(w_mlp_loaded, LOADED)
            sp.dma_start(wkv_s[0:C2B, 1, :], wkv[128:C2, :]).then_inc(w_mlp_loaded, LOADED)

            def step_a(p, j):
                s = 2 * p + j
                if ok(s + 2):
                    sp.wait_ge(A["norm_done"], 2 * s + 2)
                    load_in(s + 2, j, in_loaded)

            def step_c(p, j):
                s = 2 * p + j
                if ok(s + 2):
                    sp.wait_ge(C["in_transposed"], s + 1)
                    load_in(s + 2, j, c_loaded)
                if ok(s - 5):
                    sp.wait_ge(C["res_ready"], s - 4)
                    sp.dma_start(out[bass.ds(s - 5, 1)].rearrange("b p c -> p (b c)"), y_out[:, 1 - j, :])\
                        .then_inc(c_stored[1 - j], LOADED)

            pipeline(sp, step_a, 0, STEPS_A, behind=NB - 2)
            sp.wait_ge(A["norm_done"], 2 * NB)
            for j in range(2):
                load_in(j, j, c_loaded)
            pipeline(sp, step_c, 0, STEPS_C, behind=NB - 2)
            for j in range(2):
                sp.wait_ge(c_stored[j], NP * LOADED)

        @block.gpsimd
        def _(pool):
            nc.gpsimd.memset(ident[:, :], 0.0).then_inc(ident_ready, 1)
            nc.gpsimd.memset(minus_half[:, :], -0.5).then_inc(const_ready, 1)
            nc.gpsimd.memset(eps_t[:, :], EPS).then_inc(const_ready, 1)
            pool.wait_ge(ident_ready, 1)
            nc.gpsimd.affine_select(out=ident[:, :], in_=ident[:, :], compare_op=ALU.not_equal, fill=1.0, base=0,
                                    pattern=[[-1, 128]], channel_multiplier=1).then_inc(ident_ready, 1)
            nc.gpsimd.memset(vals[:, :, :, :], 1.0).then_inc(zero_ready, 1)

            def step_a(p, j):
                t = 2 * p + j
                if ok(t):
                    pool.wait_ge(A["stats_ready"], 2 * t + 2)
                    nc.gpsimd.tensor_tensor(var_eps[:, j, :], mean_var[:, j, 1:4:2], eps_t[:, :], ALU.add)\
                        .then_inc(A["var_ready"], 1)
                    pool.wait_ge(A["var_ready"], t + 1)
                    nc.gpsimd.tensor_tensor(rstd[:, j, :], var_eps[:, j, :], minus_half[:, 0:2], ALU.pow)\
                        .then_inc(A["rstd_ready"], 1)
                if ok(t - 1):
                    pool.wait_ge(a_qk_lo, t)
                    wait(pool, A["bias_added"], t)
                    if ok(t):
                        pool.wait_ge(A["rstd_ready"], t + 1)
                    for q in range(QUARTERS):
                        o, keys, ones = alone(1 - j, q, 1, KT)
                        last = nc.gpsimd.tensor_tensor(o, keys, ones.unsqueeze(2).unsqueeze(3).broadcast_to([32, 2, KT, TOK]),
                                                       ALU.mult)
                    last.then_inc(a_alone_pool, 1)
                    pool.wait_ge(a_alone_pool, t)
                if ok(t):
                    pool.wait_ge(A["norm_done"], 2 * t + 2)
                    if known(t) and t == 0:
                        pool.wait_ge(w_out_loaded, 3 * LOADED)
                    nc.gpsimd.tensor_tensor(tile_of(t), tile_of(t), bproj_row[:, :], ALU.add)\
                        .then_inc(A["bias_added"], 1)

            pool.wait_ge(const_ready, 2)
            pool.wait_ge(zero_ready, 1)
            at(step_a, 0)
            pool.wait_ge(rows_zeroed, 2)
            pool.wait_ge(w_b1_loaded, 6 * LOADED)
            pipeline(pool, step_a, 1, NB)

            def norm_b(p):
                pool.wait_ge(b_stats, 2 * p + 2)
                nc.gpsimd.tensor_tensor(var_eps[:, :, 0], mean_var[:, :, 1], eps_t[:, :], ALU.add).then_inc(b_var, 1)
                pool.wait_ge(b_var, p + 1)
                nc.gpsimd.tensor_tensor(rstd[:, :, 0], var_eps[:, :, 0], minus_half[:, 0:2], ALU.pow).then_inc(b_rstd, 1)
                pool.wait_ge(b_norm, 2 * p + 2)
                for j in range(2):
                    nc.gpsimd.tensor_tensor(tile_of(2 * p + j), tile_of(2 * p + j), b2_row[:, :], ALU.add).then_inc(b_bias, 1)

            norm_b(0)
            pool.wait_ge(b_bias, 2)
            at(step_a, NB)
            norm_b(1)
            pool.wait_ge(w_mlp_loaded, 6 * LOADED)
            pool.wait_ge(b_bias, 4)
            for u in range(4):
                nc.gpsimd.tensor_copy(W2_hi[:, part(u), :], W2_s[:, part(u), :]).then_inc(w2_hi_done, 1)
            pool.wait_ge(w2_hi_done, 4)
            for u in range(4):
                nc.gpsimd.tensor_tensor(W2_lo[:, part(u), :], W2_s[:, part(u), :], W2_hi[:, part(u), :].bitcast(fp32), ALU.subtract)\
                    .then_inc(w2_lo_done, 1)
            with pool.Fori(0, NP - 2) as i:
                norm_b(i + 2)

            def rstd_c(t, j):
                pool.wait_ge(C["stats_ready"], t + 1)
                nc.gpsimd.tensor_tensor(var_eps[:, j, 0:1], mean_sq[:, j, :], eps_t[:, 0:1], ALU.add)\
                    .then_inc(C["var_ready"], 1)
                pool.wait_ge(C["var_ready"], t + 1)
                nc.gpsimd.tensor_tensor(rstd[:, j, 0:1], var_eps[:, j, 0:1], minus_half[:, 0:1], ALU.pow)\
                    .then_inc(C["rstd_ready"], 1)

            def step_c(p, j):
                t = 2 * p + j
                if ok(t + 1):
                    rstd_c(t + 1, 1 - j)
                if ok(t - 1):
                    pool.wait_ge(c_norm_min, t)
                    nc.gpsimd.tensor_tensor(norm_inv[:, 1 - j, :], norm_sq_min[:, 1 - j, :], minus_half[:, :], ALU.pow)\
                        .then_inc(c_norm_inv, 1)

            rstd_c(0, 0)
            pipeline(pool, step_c, 0, STEPS_C, behind=NB - 2)

        @block.scalar
        def _(act):
            for n, v in enumerate((ln1_w, ln1_b, ln2_w, ln2_b)):
                if n < 2:
                    act.dma_start(ln_cols[:, n, :], v.rearrange("(t p) -> p t", p=128), allow_slow_non_contiguous=True).then_inc(w_att_loaded, LOADED)
                else:
                    act.dma_start(ln_cols[:, n, 0:1], v[0:128].unsqueeze(1)).then_inc(w_att_loaded, LOADED)
                    act.dma_start(ln_cols[0:C2B, n, 1:2], v[128:C2].unsqueeze(1)).then_inc(w_att_loaded, LOADED)

            def inputs_T(t, j, S):
                act.wait_ge(S["in_transposed"], t + 1)
                wait(act, S["v_mm"], t - 1)
                o = inT[:, j, :, :] if S is A else inT_r[:, j, 0, :, :]
                nc.scalar.activation(o[:, 0:3, :], bank_t[:, 0:3 * TOK].rearrange("p (a b) -> p a b", a=3), ACT.Copy)\
                    .then_inc(S["inT_ready"], 1)
                nc.scalar.activation(o[0:C2B, 3, :], bank_t[0:C2B, 3 * TOK:], ACT.Copy).then_inc(S["inT_ready"], 1)

            def out_T(f, S):
                act.wait_ge(S["av"], NG * f + NG)
                wait(act, S["o_back"], f)
                nc.scalar.activation(oT[:, :], bank_o[:, :], ACT.Copy).then_inc(S["oT_ready"], 1)

            def on_T(f, S):
                act.wait_ge(S["on_transposed"], f + 1)
                wait(act, S["proj_mm"], f)
                o = onT[:, :, :] if S is A else onT_r[:, 0, :, :]
                nc.scalar.activation(o, bank_y[:, 0:C1].rearrange("p (a b) -> p a b", a=KT), ACT.Copy)\
                    .then_inc(S["onT_ready"], 1)

            def lnT_b(p, later):
                act.wait_ge(b_T, p + 1)
                if later:
                    act.wait_ge(b_w1, 4 * p)
                nc.scalar.activation(lnT_hi[:, :, :], bank_t[:, :].rearrange("p (a b) -> p a b", a=KT), ACT.Copy)\
                    .then_inc(b_lnT_hi, 1)

            def step_a(p, j):
                s = 2 * p + j
                a = s - 2

                def exp(g):
                    if ok(a):
                        act.wait_ge(A["shifted"], NG * a + g + 1)
                        nc.scalar.activation(P[:, g, :], P[:, g, :], ACT.Exp, scale=HD ** -0.5).then_inc(A["exped"], 1)

                def weights_T(tile, g):
                    if ok(tile):
                        c = NG * tile + g
                        act.wait_ge(A["w_transposed"], c + 1)
                        wait(act, A["av"], c - 3)
                        nc.scalar.activation(PT[:, g, :], bank_s[2 + g % 2][:, :], ACT.Copy).then_inc(A["wT_ready"], 1)

                def keys_alone(quarters):
                    if ok(s - 1):
                        act.wait_ge(a_qk_lo, s)
                        for q in quarters:
                            o, keys, ones = alone(1 - j, q, 0, KT)
                            nc.scalar.activation(o, keys, ACT.Copy, scale=ones).then_inc(a_alone_act, 1)

                if ok(s - 1):
                    act.wait_ge(A["qk_ready"], s)
                    wait(act, A["scores"], NG * (s - 2))
                    nc.scalar.activation(qkT_r[:, 1 - j, 0, :, :], qkT[:, 1 - j, :, :], ACT.Copy).then_inc(a_qk_hi, 1)
                if ok(s - 4):
                    on_T(s - 4, A)
                weights_T(a - 1, 2)
                weights_T(a - 1, 3)
                exp(0)
                keys_alone((0,))
                exp(1)
                if ok(s):
                    inputs_T(s, j, A)
                elif s == NB:
                    lnT_b(0, False)
                weights_T(a, 0)
                if ok(a - 1):
                    out_T(a - 1, A)
                keys_alone((1,))
                exp(2)
                weights_T(a, 1)
                keys_alone((2, 3))
                exp(3)

            at(step_a, 0)
            act.wait_ge(zero_ready, 2)
            nc.scalar.activation(solo[:, 1, :, :, :], zero[:, :].unsqueeze(2).unsqueeze(3).broadcast_to([128, 2, H, TOK]), ACT.Copy)\
                .then_inc(rows_zeroed, 1)
            act.wait_ge(rows_zeroed, 2)
            act.wait_ge(w_b1_loaded, 6 * LOADED)
            pipeline(act, step_a, 1, STEPS_A - 2)

            def gelu_b(p, later, parts=range(4)):
                for u in parts:
                    c = 4 * p + u + 1
                    act.wait_ge(b_w1, c)
                    if later and u == 0:
                        act.wait_ge(b_w2, 2 * p)
                    for k in range(2):
                        m = 2 * u + k
                        last = nc.scalar.activation(hT[:, m, :], bank_s[u][:, 256 * k:256 * k + 256], ACT.Gelu,
                                                    bias=b1_all[:, m:m + 1])
                    last.then_inc(b_gelu, 1)
                    act.wait_ge(b_gelu, c)
                    nc.scalar.activation(hT_hi[:, part(u), :], hT[:, part(u), :], ACT.Copy).then_inc(b_hT_hi, 1)

            at(step_a, STEPS_A - 2)
            act.wait_ge(w_mlp_ready, 3)
            act.wait_ge(w1_lo_done, 4)
            at(step_a, STEPS_A - 1)
            gelu_b(0, False)
            lnT_b(1, True)
            with act.Fori(0, NP - 2) as i:
                gelu_b(i + 1, True)
                lnT_b(i + 2, True)

            def mean_square(t, j):
                wait(act, C["stats_ready"], t)
                nc.scalar.activation(x_sq[:, :], tile_of(t), ACT.Square, scale=C1 ** -0.5, accum_out=mean_sq[:, j, :])\
                    .then_inc(C["stats_ready"], 1)

            def step_c(p, j):
                s = 2 * p + j
                a = s - 3

                def exp(g):
                    if ok(a):
                        c = NG * a + g
                        act.wait_ge(C["scores"], c + 1)
                        wait(act, C["av"], c - 3)
                        nc.scalar.activation(PT[:, g, :], bank_s[g][:, :], ACT.Exp, scale=HD ** 0.5).then_inc(C["exped"], 1)

                def queries_alone(quarters):
                    if ok(s - 2):
                        act.wait_ge(c_unit_lo, s - 1)
                        for q in quarters:
                            o, queries, ones = alone(j, q, 1, 0)
                            nc.scalar.activation(o, queries, ACT.Copy, scale=ones).then_inc(c_alone_act, 1)

                if ok(a - 1):
                    out_T(a - 1, C)
                if ok(s - 2):
                    act.wait_ge(C["v_mm"], s - 1)
                    wait(act, C["av"], NG * (s - 3))
                    nc.scalar.activation(vals[:, j, :, 0:HD], heads(bank_t[:, 0:C1]), ACT.Copy).then_inc(C["v_ready"], 1)
                if ok(s + 1):
                    mean_square(s + 1, 1 - j)
                exp(0)
                if ok(s - 1):
                    act.wait_ge(c_rot, s)
                    wait(act, c_norm_sq, s - 1)
                    nc.scalar.activation(rot_sq[:, :], rot[:, 1 - j, :], ACT.Square).then_inc(c_rot_sq, 1)
                exp(1)
                if ok(s - 2):
                    act.wait_ge(c_turned, s - 1)
                    wait(act, C["scores"], NG * (s - 3))
                    nc.scalar.activation(qkT_r[:, j, 0, :, :], bank_qk[:, :].rearrange("p (a b) -> p a b", a=4), ACT.Copy)\
                        .then_inc(c_unit_hi, 1)
                if ok(s):
                    inputs_T(s, j, C)
                exp(2)
                queries_alone((0, 1))
                exp(3)
                if ok(a - 1):
                    on_T(a - 1, C)
                queries_alone((2, 3))

            act.wait_ge(b_x, NB - 4)
            mean_square(0, 0)
            at(step_c, 0)
            gelu_b(NP - 1, True, [0])
            at(step_c, 1)
            gelu_b(NP - 1, True, [1, 2, 3])
            at(step_c, 2)
            act.wait_ge(b_x, NB)
            pipeline(act, step_c, 3, STEPS_C, behind=NB - 2)

        @block.tensor
        def _(pe):
            mm = nc.tensor.matmul
            rows = (128, C2B)

            def attention_biases():
                pe.wait_ge(w_att_loaded, 9 * LOADED)
                pe.wait_ge(wide_ready, 2)
                for m in range(KT):
                    for k in range(KT):
                        mm(bank_y[:, C1 + m:C1 + m + 1], Wq_s[:, k, 128 * m:128 * m + 128], ln_cols[:, 1, k:k + 1],
                           start=k == 0, stop=k == KT - 1)
                for m in range(KT):
                    for k, r in enumerate(rows):
                        mm(bank_y[:, C1 + 2 + m:C1 + 3 + m], Wkv_s[0:r, k, 128 * m:128 * m + 128], ln_cols[0:r, 3, k:k + 1],
                           start=k == 0, stop=k == 1)
                for k, r in enumerate(rows):
                    last = mm(bank_y[:, 0:C1], ln2b_wide[0:r, k, :], Wkv_s[0:r, k, C1:], start=k == 0, stop=k == 1)
                last.then_inc(bias_mm, 1)

            def mlp_bias(parts):
                pe.wait_ge(w_mlp_loaded, 6 * LOADED)
                pe.wait_ge(w_b1_loaded, 6 * LOADED)
                for m in parts:
                    for k in range(KT):
                        last = mm(bank_t[:, C1 + m:C1 + m + 1], W1_s[:, k, 128 * m:128 * m + 128], ln_cols[:, 5, k:k + 1],
                                  start=k == 0, stop=k == KT - 1)
                last.then_inc(bias_mm, 1)

            def inputs_T(j, xs, ys, S):
                for k in range(KT):
                    nc.tensor.transpose(bank_t[:, 128 * k:128 * k + 128], xs[:, j, 128 * k:128 * k + 128], ident[:, :])
                nc.tensor.transpose(bank_t[:, 256:384], ys[:, j, 0:128], ident[:, :])
                nc.tensor.transpose(bank_t[0:C2B, 384:512], ys[:, j, 128:C2], ident[:, :]).then_inc(S["in_transposed"], 1)

            def split_mm(out, a, b, sizes=(128, 128)):
                for k, r in enumerate(sizes):
                    for n, (x, y) in enumerate(HI_LO):
                        last = mm(out, a[0:r, x, k, :], b[0:r, y, k, :], start=k == n == 0, stop=k == 1 and n == 2)
                return last


            def weighted(a, g, j, S):
                if not ok(a):
                    return
                pe.wait_ge(S["wT_ready"] if S is A else S["exped"], NG * a + g + 1)
                if g == 0:
                    pe.wait_ge(S["v_ready"], a + 1)
                    wait(pe, S["oT_ready"], a)
                for r in range(GH):
                    last = mm(bank_o[32 * r:32 * r + VW, 128 * g:128 * g + 128], vals[:, j, GH * g + r, :],
                              PT[:, g, 128 * r:128 * r + 128], start=True, stop=True)
                last.then_inc(S["av"], 1)

            def back(f, S):
                if ok(f):
                    pe.wait_ge(S["oT_ready"], f + 1)
                    wait(pe, S["res_ready"], f)
                    for g in range(NG):
                        last = nc.tensor.transpose(bank_y[:, 128 * g:128 * g + 128], oT[:, 128 * g:128 * g + 128], ident[:, :])
                    last.then_inc(S["o_back"], 1)

            def normed_T(f, S):
                if ok(f):
                    pe.wait_ge(S["on_ready"], f + 1)
                    for k in range(KT):
                        last = nc.tensor.transpose(bank_y[:, 128 * k:128 * k + 128], on[:, 128 * k:128 * k + 128], ident[:, :])
                    last.then_inc(S["on_transposed"], 1)

            def project(f, S):
                if ok(f):
                    pe.wait_ge(S["onT_ready"], f + 1)
                    if S is A:
                        for k in range(KT):
                            last = mm(bank_y[:, 0:C1], onT[:, k, :], Wproj_s[:, k, :], start=k == 0, stop=k == KT - 1)
                    else:
                        pe.wait_ge(c_onT_lo, f + 1)
                        last = split_mm(bank_y[:, 0:C1], onT_r[:, :, :, :], wout_r[:, :, :, :])
                    last.then_inc(S["proj_mm"], 1)

            def turn_b(p):
                pe.wait_ge(b_norm, 2 * p + 2)
                for k in range(KT):
                    for j in range(2):
                        n = 2 * k + j
                        last = nc.tensor.transpose(bank_t[:, 128 * n:128 * n + 128], xn[:, j, 128 * k:128 * k + 128], ident[:, :])
                last.then_inc(b_T, 1)

            def step_a(p, j):
                s = 2 * p + j
                a, i = s - 2, 1 - j

                def score(g):
                    if ok(a):
                        c = NG * a + g
                        if g == 0:
                            pe.wait_ge(a_alone_act, QUARTERS * (a + 1))
                            pe.wait_ge(a_alone_pool, a + 1)
                        wait(pe, A["shifted"], c - 1)
                        for n, (q, k) in enumerate(HI_LO):
                            last = mm(bank_s[g % 2][:, :], qkT_r[:, j, q, g // 2, :], solo[:, j, k, GH * g:GH * g + GH, :],
                                      start=n == 0, stop=n == 2)
                        last.then_inc(A["scores"], 1)

                def weights_T(tile, g):
                    if ok(tile):
                        c = NG * tile + g
                        pe.wait_ge(A["exped"], c + 1)
                        wait(pe, A["wT_ready"], c - 1)
                        for r in range(GH):
                            last = nc.tensor.transpose(bank_s[2 + g % 2][:, 128 * r:128 * r + 128],
                                                       P[:, g, 128 * r:128 * r + 128], ident[:, :])
                        last.then_inc(A["w_transposed"], 1)

                if ok(s - 1):
                    pe.wait_ge(A["inT_ready"], 2 * s)
                    wait(pe, A["qk_ready"], s - 1)
                    for m in range(KT):
                        for k in range(KT):
                            mm(bank_qk[:, 128 * m:128 * m + 128], Wq_n[:, k, 128 * m:128 * m + 128], inT[:, i, k, :],
                               start=k == 0, stop=k == KT - 1)
                    for m in range(KT):
                        for k, r in enumerate(rows):
                            last = mm(bank_qk[:, 256 + 128 * m:384 + 128 * m], Wkv_n[0:r, k, 128 * m:128 * m + 128],
                                      inT[0:r, i, 2 + k, :], start=k == 0, stop=k == 1)
                    last.then_inc(A["qk_mm"], 1)
                score(0)
                normed_T(s - 4, A)
                weights_T(a - 1, 2)
                weighted(a - 1, 1, i, A)
                score(1)
                weights_T(a - 1, 3)
                project(s - 4, A)
                weighted(a - 1, 2, i, A)
                score(2)
                if ok(s):
                    pe.wait_ge(A["norm_done"], 2 * s + 2)
                    wait(pe, A["v_ready"], s - 1)
                    inputs_T(j, xn, yn, A)
                elif s in (NB, NB + 1):
                    pe.wait_ge(A["v_ready"], s - 1)
                    turn_b(s - NB)
                weights_T(a, 0)
                weighted(a - 1, 3, i, A)
                score(3)
                weights_T(a, 1)
                if ok(s - 1):
                    if ok(s):
                        pe.wait_ge(A["inT_ready"], 2 * s + 2)
                    else:
                        pe.wait_ge(b_lnT_lo, 1)
                    for k, r in enumerate(rows):
                        last = mm(bank_t[:, 0:C1], inT[0:r, i, 2 + k, :], Wkv_n[0:r, k, C1:], start=k == 0, stop=k == 1)
                    last.then_inc(A["v_mm"], 1)
                if known(s) and s in bias_parts:
                    mlp_bias(bias_parts[s])
                back(a - 1, A)
                weighted(a, 0, j, A)

            pe.wait_ge(ident_ready, 2)
            at(step_a, 0)
            attention_biases()
            pe.wait_ge(w_att_ready, 2)
            at(step_a, 1)
            pe.wait_ge(w_out_loaded, 3 * LOADED)
            pe.wait_ge(w_att_ready, 4)
            pipeline(pe, step_a, 2, STEPS_A - 2)

            def up_b(p, later, parts=range(4)):
                for u in parts:
                    if u == 0:
                        pe.wait_ge(b_lnT_hi, p + 1)
                        pe.wait_ge(b_lnT_lo, p + 1)
                    if later:
                        pe.wait_ge(b_gelu, 4 * p + u - 3)
                    for m in (2 * u, 2 * u + 1):
                        for k in range(KT):
                            for n, (w, act_T) in enumerate(((W1_hi, lnT_hi), (W1_hi, lnT_lo), (W1_lo, lnT_hi))):
                                last = mm(bank_s[u][:, 256 * (m % 2):256 * (m % 2) + 256], w[:, k, 128 * m:128 * m + 128],
                                          act_T[:, k, :], start=k == n == 0, stop=k == KT - 1 and n == 2)
                    last.then_inc(b_w1, 1)

            def down_b(p, later):
                for parts in (range(0, 3), range(3, 4)):
                    for j, bank in enumerate((bank_o, bank_y)):
                        if later and parts[0] == 0:
                            pe.wait_ge(b_x, 2 * p + j - 1)
                        for u in parts:
                            if j == 0:
                                pe.wait_ge(b_hT_lo, 4 * p + u + 1)
                            for m in (2 * u, 2 * u + 1):
                                for n, (h, w) in enumerate(((hT_hi, W2_hi), (hT_hi, W2_lo), (hT_lo, W2_hi))):
                                    last = mm(bank[:, 0:C1], h[:, m, 128 * j:128 * j + 128], w[:, m, :],
                                              start=m == n == 0, stop=m == HM - 1 and n == 2)
                        if parts[-1] == 3:
                            last.then_inc(b_w2, 1)

            at(step_a, STEPS_A - 2)
            pe.wait_ge(w1_lo_done, 2)
            pe.wait_ge(A["shifted"], NG * NB)
            up_b(0, False, [0])
            normed_T(NB - 1, A)
            up_b(0, False, [1])
            project(NB - 1, A)
            pe.wait_ge(w1_lo_done, 4)
            pe.wait_ge(A["wT_ready"], NG * NB)
            up_b(0, False, [2, 3])
            pe.wait_ge(w2_lo_done, 4)
            pe.wait_ge(A["oT_ready"], NB)
            pe.wait_ge(A["res_ready"], NB)
            down_b(0, False)
            with pe.Fori(0, NP - 2) as i:
                up_b(i + 1, True)
                turn_b(i + 2)
                down_b(i + 1, True)

            def step_c(p, j):
                s = 2 * p + j
                a, i = s - 3, 1 - j

                def score(g):
                    if ok(a):
                        c = NG * a + g
                        if g == 0:
                            pe.wait_ge(c_alone_act, QUARTERS * (a + 1))
                            pe.wait_ge(c_alone_dve, QUARTERS * (a + 1))
                        wait(pe, C["exped"], c - 3)
                        for n, (k, q) in enumerate(HI_LO):
                            last = mm(bank_s[g][:, :], qkT_r[:, i, k, KT + g // 2, :], solo[:, i, q, GH * g:GH * g + GH, :],
                                      start=n == 0, stop=n == 2)
                        last.then_inc(C["scores"], 1)

                if ok(s - 1):
                    pe.wait_ge(c_inT_lo, 2 * s)
                    wait(pe, c_unit_lo, s - 2)
                    split_mm(bank_qk[:, 0:C1], inT_r[:, i, :, 0:2, :], wq_r[:, :, :, :])
                    split_mm(bank_qk[:, C1:], inT_r[:, i, :, 2:4, :], wkv_r[:, :, :, 0:C1], rows).then_inc(C["qk_mm"], 1)
                weighted(a - 1, 3, j, C)
                if ok(s - 2):
                    wait(pe, c_inT_lo, 2 * s if ok(s - 1) else 2 * s - 2)
                    split_mm(bank_t[:, 0:C1], inT_r[:, j, :, 2:4, :], wkv_r[:, :, :, C1:], rows).then_inc(C["v_mm"], 1)
                project(s - 5, C)
                score(0)
                score(1)
                weighted(a, 0, i, C)
                if ok(s - 2):
                    pe.wait_ge(c_unit, s - 1)
                    wait(pe, c_rope, 2 * s if ok(s - 1) else 2 * s - 2)
                    for n in range(4):
                        last = nc.tensor.transpose(bank_qk[:, 128 * n:128 * n + 128], qk_unit[:, 128 * n:128 * n + 128], ident[:, :])
                    last.then_inc(c_turned, 1)
                back(a - 1, C)
                if ok(s):
                    pe.wait_ge(C["norm_done"], s + 1)
                    pe.wait_ge(c_loaded[j], LOADED * (p + 1))
                    wait(pe, C["v_ready"], s - 1)
                    inputs_T(j, xn, ctx_in, C)
                score(2)
                weighted(a, 1, i, C)
                score(3)
                normed_T(a - 1, C)
                weighted(a, 2, i, C)

            pe.wait_ge(wc_lo, 5)
            pe.wait_ge(b_lnT_lo, NP)
            at(step_c, 0)
            up_b(NP - 1, True, [0])
            at(step_c, 1)
            up_b(NP - 1, True, [1, 2, 3])
            down_b(NP - 1, True)
            at(step_c, 2)
            pe.wait_ge(b_x, NB)
            pe.wait_ge(b_gelu, 4 * NP)
            pipeline(pe, step_c, 3, STEPS_C)

        @block.vector
        def _(dve):
            v = nc.vector
            v.memset(zero[:, :], 0.0).then_inc(zero_ready, 1)
            v.memset(bank_o[:, :], 0.0).then_inc(wide_ready, 1)
            dve.wait_ge(zero_ready, 2)
            v.tensor_copy(solo[:, 0, :, :, :], zero[:, :].unsqueeze(2).unsqueeze(3).broadcast_to([128, 2, H, TOK]))\
                .then_inc(rows_zeroed, 1)

            def attention_weights():
                dve.wait_ge(w_att_loaded, 9 * LOADED)
                for k, r in enumerate((128, C2B)):
                    last = v.tensor_copy(ln2b_wide[0:r, k, :], ln_cols[0:r, 3, k:k + 1].broadcast_to([r, 128]))
                last.then_inc(wide_ready, 1)
                for k in range(KT):
                    last = v.tensor_scalar(Wq_n[:, k, :], Wq_s[:, k, :], ln_cols[:, 0, k:k + 1], None, ALU.mult)
                last.then_inc(w_att_ready, 1)
                for k, r in enumerate((128, C2B)):
                    last = v.tensor_scalar(Wkv_n[0:r, k, :], Wkv_s[0:r, k, :], ln_cols[0:r, 2, k:k + 1], None, ALU.mult)
                last.then_inc(w_att_ready, 1)
                dve.wait_ge(bias_mm, 1)
                v.tensor_copy(qk_bias[:, :], bank_y[:, C1:C1 + 4]).then_inc(w_att_ready, 1)
                v.tensor_copy(v_bias[:, :], bank_y[:, 0:C1]).then_inc(w_att_ready, 1)

            def w1_split(u):
                if u == 0:
                    dve.wait_ge(w_mlp_loaded, 6 * LOADED)
                scale = ln_cols[:, 4, u % 2:u % 2 + 1]
                v.tensor_scalar(w1_part(W1_hi, u), w1_part(W1_s, u), scale, None, ALU.mult).then_inc(w1_hi_done, 1)
                dve.wait_ge(w1_hi_done, u + 1)
                v.scalar_tensor_tensor(w1_part(W1_lo, u), w1_part(W1_s, u), scale, w1_part(W1_hi, u).bitcast(fp32),
                                       ALU.mult, ALU.subtract).then_inc(w1_lo_done, 1)

            def values(t, j, S):
                dve.wait_ge(S["v_mm"], t + 1)
                wait(dve, S["av"], NG * (t - 1))
                v.tensor_tensor(vals[:, j, :, 0:HD], heads(bank_t[:, 0:C1]), heads(v_bias[:, :]), ALU.add)\
                    .then_inc(S["v_ready"], 1)

            def normalise_heads(f, S):
                o = bank_y[:, :].rearrange("p (h d) -> p h d", h=H)
                dve.wait_ge(S["o_back"], f + 1)
                v.reciprocal(row_sums_inv[:, :], o[:, :, HD]).then_inc(S["recip"], 1)
                dve.wait_ge(S["recip"], f + 1)
                wait(dve, S["on_transposed"], f)
                v.tensor_tensor(heads(on[:, :]), o[:, :, 0:HD], each(row_sums_inv[:, :], H, HD), ALU.mult)\
                    .then_inc(S["on_ready"], 1)

            def stats_b(p):
                for j in range(2):
                    v.bn_stats(stats[:, j, 0:6], tile_of(2 * p + j)).then_inc(b_stats_raw, 1)
                dve.wait_ge(b_stats_raw, 2 * p + 2)
                v.tensor_copy(wait_carrier[:, :], stats[:, 0, 0:1])
                for j in range(2):
                    v.bn_aggr(mean_var[:, j, 0:2], stats[:, j, 0:6]).then_inc(b_stats, 1)

            def normalise_b(p, later):
                dve.wait_ge(b_stats, 2 * p + 2)
                dve.wait_ge(b_rstd, p + 1)
                if later:
                    dve.wait_ge(b_T, p)
                for j in range(2):
                    v.tensor_scalar(xn[:, j, :], tile_of(2 * p + j), mean_var[:, j, 0:1], rstd[:, j, 0:1],
                                    ALU.subtract, ALU.mult).then_inc(b_norm, 1)

            def split_lnT(p):
                dve.wait_ge(b_lnT_hi, p + 1)
                v.tensor_tensor(lnT_lo[:, :, :], bank_t[:, :].rearrange("p (a b) -> p a b", a=KT), lnT_hi[:, :, :].bitcast(fp32),
                                ALU.subtract).then_inc(b_lnT_lo, 1)

            def step_a(p, j):
                s = 2 * p + j
                a, i = s - 2, 1 - j

                def maximum(g):
                    if ok(a):
                        dve.wait_ge(A["scores"], NG * a + g + 1)
                        v.tensor_reduce(row_max[:, g, :], heads(bank_s[g % 2][:, :], GH), AX.X, ALU.max).then_inc(A["maxed"], 1)

                def shift(g):
                    if ok(a):
                        c = NG * a + g
                        dve.wait_ge(A["maxed"], c + 1)
                        wait(dve, A["w_transposed"], c - 3)
                        v.tensor_tensor(heads(P[:, g, :], GH), heads(bank_s[g % 2][:, :], GH), each(row_max[:, g, :], GH, TOK),
                                        ALU.subtract).then_inc(A["shifted"], 1)

                if ok(s):
                    dve.wait_ge(in_loaded[j], 2 * LOADED * (p + 1))
                    v.bn_stats(stats[:, j, 0:6], tile_of(s)).then_inc(A["stats_raw"], 1)
                    v.bn_stats(stats[:, j, 6:12], ctx_in[:, j, :]).then_inc(A["stats_raw"], 1)
                    dve.wait_ge(A["stats_raw"], 2 * s + 2)
                    v.tensor_copy(wait_carrier[:, :], stats[:, j, 0:1])
                    v.bn_aggr(mean_var[:, j, 0:2], stats[:, j, 0:6]).then_inc(A["stats_ready"], 1)
                    v.bn_aggr(mean_var[:, j, 2:4], stats[:, j, 6:12]).then_inc(A["stats_ready"], 1)
                elif s in (NB, NB + 1):
                    stats_b(s - NB)
                if known(s) and s - 1 in bias_parts:
                    parts = bias_parts[s - 1]
                    dve.wait_ge(bias_mm, s - 1)
                    v.tensor_tensor(b1_all[:, parts[0]:parts[-1] + 1], bank_t[:, C1 + parts[0]:C1 + parts[-1] + 1],
                                    b1_cols[:, parts[0]:parts[-1] + 1], ALU.add).then_inc(w_mlp_ready, 1)
                if ok(s - 2):
                    values(s - 2, j, A)
                if ok(s - 1):
                    dve.wait_ge(A["qk_mm"], s)
                    v.tensor_tensor(qkT[:, i, :, :], bank_qk[:, :].rearrange("p (a b) -> p a b", a=4),
                                    each(qk_bias[:, :], 4, TOK), ALU.add).then_inc(A["qk_ready"], 1)
                if ok(s):
                    dve.wait_ge(A["stats_ready"], 2 * s + 2)
                    dve.wait_ge(A["rstd_ready"], s + 1)
                    wait(dve, A["in_transposed"], s - 1)
                    v.tensor_scalar(xn[:, j, :], tile_of(s), mean_var[:, j, 0:1], rstd[:, j, 0:1],
                                    ALU.subtract, ALU.mult).then_inc(A["norm_done"], 1)
                    v.tensor_scalar(yn[:, j, :], ctx_in[:, j, :], mean_var[:, j, 2:3], rstd[:, j, 1:2],
                                    ALU.subtract, ALU.mult).then_inc(A["norm_done"], 1)
                elif s in (NB, NB + 1):
                    if s == NB:
                        dve.wait_ge(A["in_transposed"], NB)
                    normalise_b(s - NB, s > NB)
                maximum(0)
                if ok(s - 1):
                    dve.wait_ge(a_qk_hi, s)
                    v.tensor_tensor(qkT_r[:, i, 1, :, :], qkT[:, i, :, :], qkT_r[:, i, 0, :, :].bitcast(fp32), ALU.subtract)\
                        .then_inc(a_qk_lo, 1)
                shift(0)
                maximum(1)
                shift(1)
                maximum(2)
                if ok(s - 4):
                    dve.wait_ge(A["proj_mm"], s - 3)
                    dve.wait_ge(A["bias_added"], s - 3)
                    v.tensor_tensor(tile_of(s - 4), tile_of(s - 4), bank_y[:, 0:C1], ALU.add).then_inc(A["res_ready"], 1)
                shift(2)
                if known(s) and s == NB:
                    split_lnT(0)
                maximum(3)
                shift(3)
                if ok(a - 1):
                    normalise_heads(a - 1, A)

            at(step_a, 0)
            attention_weights()
            dve.wait_ge(w_att_ready, 4)
            dve.wait_ge(w_b1_loaded, 6 * LOADED)
            at(step_a, 1)
            w1_split(0)
            w1_split(1)
            pipeline(dve, step_a, 2, STEPS_A - 2)
            w1_split(2)
            w1_split(3)
            at(step_a, STEPS_A - 2, STEPS_A - 1)

            def res_b(p):
                for j, bank in enumerate((bank_o, bank_y)):
                    dve.wait_ge(b_w2, 2 * p + j + 1)
                    dve.wait_ge(b_bias, 2 * p + j + 1)
                    v.tensor_tensor(tile_of(2 * p + j), tile_of(2 * p + j), bank[:, 0:C1], ALU.add).then_inc(b_x, 1)

            def split_hT(p, parts=range(4)):
                for u in parts:
                    dve.wait_ge(b_hT_hi, 4 * p + u + 1)
                    v.tensor_tensor(hT_lo[:, part(u), :], hT[:, part(u), :], hT_hi[:, part(u), :].bitcast(fp32),
                                    ALU.subtract).then_inc(b_hT_lo, 1)

            dve.wait_ge(A["res_ready"], NB)
            split_hT(0)
            split_lnT(1)
            res_b(0)

            def pair_b(n):
                stats_b(n + 1)
                normalise_b(n + 1, True)
                split_hT(n)
                split_lnT(n + 1)

            def split(hi, lo, w, count):
                v.tensor_copy(hi, w).then_inc(wc_hi, 1)
                dve.wait_ge(wc_hi, count)
                v.tensor_tensor(lo, w, hi.bitcast(fp32), ALU.subtract).then_inc(wc_lo, 1)

            for k in range(KT):
                scale = ln_cols[:, 6, k:k + 1]
                v.tensor_scalar(wq_r[:, 0, k, :], wq_s[:, k, :], scale, None, ALU.mult).then_inc(wc_hi, 1)
                dve.wait_ge(wc_hi, k + 1)
                v.scalar_tensor_tensor(wq_r[:, 1, k, :], wq_s[:, k, :], scale, wq_r[:, 0, k, :].bitcast(fp32),
                                       ALU.mult, ALU.subtract).then_inc(wc_lo, 1)
            split(wout_r[:, 0], wout_r[:, 1], wout_s[:, :, :], 3)
            with dve.Fori(0, NP - 3) as i:
                pair_b(i + 1)
                res_b(i + 1)
            for k, r in enumerate((128, C2B)):
                split(wkv_r[0:r, 0, k, :], wkv_r[0:r, 1, k, :], wkv_s[0:r, k, :], 4 + k)
            pair_b(NP - 2)
            dve.wait_ge(b_T, NP)
            dve.wait_ge(b_x, NB - 4)

            def normalise_c(p, j):
                s = 2 * p + j
                dve.wait_ge(C["stats_ready"], s + 1)
                dve.wait_ge(C["rstd_ready"], s + 1)
                wait(dve, C["in_transposed"], s - 1)
                v.tensor_scalar(xn[:, j, :], tile_of(s), rstd[:, j, 0:1], None, ALU.mult).then_inc(C["norm_done"], 1)

            def split_inT(p, j):
                s = 2 * p + j
                dve.wait_ge(C["inT_ready"], 2 * s + 2)
                v.tensor_tensor(inT_r[:, j, 1, 0:3, :], bank_t[:, 0:3 * TOK].rearrange("p (a b) -> p a b", a=3),
                                inT_r[:, j, 0, 0:3, :].bitcast(fp32), ALU.subtract).then_inc(c_inT_lo, 1)
                v.tensor_tensor(inT_r[0:C2B, j, 1, 3, :], bank_t[0:C2B, 3 * TOK:], inT_r[0:C2B, j, 0, 3, :].bitcast(fp32),
                                ALU.subtract).then_inc(c_inT_lo, 1)

            def queries_alone(p, j, quarters):
                s = 2 * p + j
                if ok(s - 2):
                    dve.wait_ge(c_unit_lo, s - 1)
                    for q in quarters:
                        o, queries, ones = alone(j, q, 0, 0)
                        v.tensor_scalar(o, queries, ones, None, ALU.mult).then_inc(c_alone_dve, 1)

            def step_c(p, j, normalised=False):
                s = 2 * p + j
                i = 1 - j
                if ok(s - 1):
                    dve.wait_ge(C["qk_mm"], s)
                    cos = rope_t[:, 0, :].unsqueeze(1).broadcast_to([128, 2 * H, HD])
                    sin = rope_t[:, 1, :].rearrange("p (s d) -> p s d", s=2).unsqueeze(1).broadcast_to([128, 2 * H, 2, HD // 2])
                    swapped = bank_qk[:, :].rearrange("p (h s d) -> p h s d", s=2, d=HD // 2)[:, :, ::-1, :]
                    v.tensor_tensor(heads(rot_a[:, :], 2 * H), heads(bank_qk[:, :], 2 * H), cos, ALU.mult).then_inc(c_rope, 1)
                    v.tensor_tensor(rot_b[:, :].rearrange("p (h s d) -> p h s d", s=2, d=HD // 2), swapped, sin, ALU.mult)\
                        .then_inc(c_rope, 1)
                    dve.wait_ge(c_rope, 2 * s)
                    v.tensor_tensor(rot[:, i, :], rot_a[:, :], rot_b[:, :], ALU.add).then_inc(c_rot, 1)
                if ok(s - 2):
                    dve.wait_ge(c_norm_inv, s - 1)
                    wait(dve, c_turned, s - 2)
                    v.tensor_tensor(heads(qk_unit[:, :], 2 * H), heads(rot[:, j, :], 2 * H),
                                    each(norm_inv[:, j, :], 2 * H, HD), ALU.mult).then_inc(c_unit, 1)
                if ok(s - 5):
                    dve.wait_ge(C["proj_mm"], s - 4)
                    wait(dve, c_stored[i], LOADED * (p - 2 if j else p - 3))
                    v.tensor_tensor(y_out[:, i, :], tile_of(s - 5), bank_y[:, 0:C1], ALU.add).then_inc(C["res_ready"], 1)
                if ok(s) and not normalised:
                    normalise_c(p, j)
                if ok(s - 1):
                    dve.wait_ge(c_rot_sq, s)
                    v.tensor_reduce(norm_sq[:, i, :], heads(rot_sq[:, :], 2 * H), AX.X, ALU.add).then_inc(c_norm_sq, 1)
                    dve.wait_ge(c_norm_sq, s)
                    v.tensor_scalar(norm_sq_min[:, i, :], norm_sq[:, i, :], EPS_L2 ** 2, None, ALU.max).then_inc(c_norm_min, 1)
                if ok(s - 2):
                    dve.wait_ge(c_unit_hi, s - 1)
                    v.tensor_tensor(qkT_r[:, j, 1, :, :], bank_qk[:, :].rearrange("p (a b) -> p a b", a=4),
                                    qkT_r[:, j, 0, :, :].bitcast(fp32), ALU.subtract).then_inc(c_unit_lo, 1)
                if ok(s - 4):
                    normalise_heads(s - 4, C)
                if ok(s):
                    split_inT(p, j)
                queries_alone(p, j, range(QUARTERS))
                if ok(s - 4):
                    dve.wait_ge(C["onT_ready"], s - 3)
                    v.tensor_tensor(onT_r[:, 1, :, :], bank_y[:, 0:C1].rearrange("p (a b) -> p a b", a=KT),
                                    onT_r[:, 0, :, :].bitcast(fp32), ALU.subtract).then_inc(c_onT_lo, 1)

            normalise_c(0, 0)
            split_inT(0, 0)
            res_b(NP - 2)
            normalise_c(0, 1)
            split_hT(NP - 1, [0])
            step_c(0, 1, True)
            split_hT(NP - 1, [1, 2, 3])
            res_b(NP - 1)
            dve.wait_ge(b_x, NB)
            pipeline(dve, step_c, 2, STEPS_C, peeled=8)


_INS = ['x', 'ctx_768', 'L0_xattn_ln1_w', 'L0_xattn_ln1_b', 'L0_xattn_ln2_w', 'L0_xattn_ln2_b', 'L0_xattn_ln3_w',
        'L0_xattn_ln3_b', 'L0_xattn_Wq', 'L0_xattn_Wkv', 'L0_xattn_Wproj', 'L0_xattn_bproj', 'L0_xattn_W1',
        'L0_xattn_b1', 'L0_xattn_W2', 'L0_xattn_b2', 'L1_xattn_norm_w', 'L1_xattn_wq', 'L1_xattn_wkv', 'L1_xattn_wout']


def kernel(**inputs):
    import numpy as np
    import concourse.bacc as bacc
    from concourse.bass_utils import run_bass_kernel_spmd

    nc = bacc.Bacc("TRN2", target_bir_lowering=False, num_devices=1)
    arrays, args = {}, []
    for name in _INS:
        a = np.ascontiguousarray(inputs[name])
        arrays[f"in_{name}"] = a
        args.append(nc.dram_tensor(f"in_{name}", a.shape, mybir.dt.from_np(a.dtype), kind="ExternalInput").ap())
    inv_freq = 1.0 / 10000.0 ** (np.arange(0, HD, 2, dtype=np.float32) / HD)
    angles = np.einsum('i,j->ij', np.arange(TOK, dtype=np.float32), inv_freq)
    rope = np.stack([np.cos(np.concatenate([angles, angles], -1)),
                     np.concatenate([-np.sin(angles), np.sin(angles)], -1)], 1).astype(np.float32)
    arrays["in_rope"] = rope
    args.append(nc.dram_tensor("in_rope", rope.shape, fp32, kind="ExternalInput").ap())
    halves = np.repeat(np.tile(np.eye(2, dtype=np.float32), (4, 1)), HD, 0)
    arrays["in_halves"] = halves
    args.append(nc.dram_tensor("in_halves", halves.shape, fp32, kind="ExternalInput").ap())
    out = nc.dram_tensor("out_0", (NB, TOK, C1), fp32, kind="ExternalOutput").ap()
    build(nc, *args, out)
    r = run_bass_kernel_spmd(nc, [arrays], core_ids=[0])
    return r.results[0]["out_0"]
```
